# Optimizing a Trainium2 kernel written in Bass

```python
import numpy as np
import jax
import jax.numpy as jnp

def _softmax(x, axis=-1):
    return jax.nn.softmax(x, axis=axis)

def _gelu(x):
    return jax.nn.gelu(x, approximate=True)

def _silu(x):
    return jax.nn.silu(x)

def _sigmoid(x):
    return jax.nn.sigmoid(x)

def _layernorm(x, axis=-1, eps=1e-05):
    m = jnp.mean(x, axis=axis, keepdims=True)
    v = jnp.var(x, axis=axis, keepdims=True)
    return (x - m) / jnp.sqrt(v + eps)

def _scatter_add(tgt, idx, src, axis=0):
    return tgt.at[idx].add(src)

def _segment_sum(src, seg, n):
    return jax.ops.segment_sum(src, seg, n)
kernel_name = 'mk_gnn_resnorm_d4_gnn_r8_64c838'

def setup_inputs(seed: int=0):
    np.random.seed(seed)
    _w = jnp.asarray

    def _rec_inputs():
        import jax
        import jax.numpy as jnp
        _gk = jax.random.key(seed)
        x = -0.0005121 + 1.001 * jax.random.normal(jax.random.fold_in(_gk, 1), (12500, 32), jnp.float32)
        src = jax.random.randint(jax.random.fold_in(_gk, 2), (200000,), 0, 12500, jnp.int32)
        dst = jax.random.randint(jax.random.fold_in(_gk, 3), (200000,), 0, 12500, jnp.int32)
        _o = jnp.argsort(dst, stable=True)
        src = src[_o]
        dst = dst[_o]
        edge_attr_10 = jax.random.uniform(jax.random.fold_in(_gk, 12), (200000, 10), jnp.float32, 0.0, 1)
        edge_attr_3 = 0.00109039 + 0.999626 * jax.random.normal(jax.random.fold_in(_gk, 13), (200000, 3), jnp.float32)
        edge_weight = -0.000414295 + 0.999828 * jax.random.normal(jax.random.fold_in(_gk, 15), (200000,), jnp.float32)
        return (x, src, dst, edge_attr_10, edge_attr_3, edge_weight)
    x, src, dst, edge_attr_10, edge_attr_3, edge_weight = _rec_inputs()

    def _L0_gnn_setup():
        import jax, jax.numpy as jnp
        import numpy as np
        key = jax.random.key(seed)
        k1, k2, k3 = jax.random.split(key, 3)
        N, E, D = (12500, 200000, 32)
        node_feat = jax.random.normal(k1, (N, D), dtype=jnp.float32)
        edge_attr = jax.random.normal(k2, (E,), dtype=jnp.float32)
        edge_index = jax.random.randint(k3, (2, E), 0, N, dtype=jnp.int64)
        return {'node_feat': node_feat, 'edge_attr': edge_attr, 'edge_index': edge_index, 'num_nodes': N}
    _L0_gnn_all = _L0_gnn_setup()
    _L0_gnn_in = {k: v for k, v in _L0_gnn_all.items() if k in ()}
    del _L0_gnn_all

    def _L1_gnn_setup():
        import jax, jax.numpy as jnp
        import numpy as np
        N_NODES = 6250
        N_EDGES = 200000
        IN_FEATS = 32
        HIDDEN = 48
        OUT_FEATS = 32
        RRELU_SLOPE = (1.0 / 8.0 + 1.0 / 3.0) / 2.0

        def gcn_conv(x, src, dst, W, b, num_nodes):
            loop = jnp.arange(num_nodes, dtype=src.dtype)
            s = jnp.concatenate([src, loop])
            d = jnp.concatenate([dst, loop])
            ew = jnp.ones(s.shape[0], dtype=x.dtype)
            deg = jax.ops.segment_sum(ew, d, num_segments=num_nodes)
            dinv = jnp.where(deg > 0, deg ** (-0.5), 0.0)
            norm = dinv[s] * ew * dinv[d]
            h = x @ W
            msg = h[s] * norm[:, None]
            out = jax.ops.segment_sum(msg, d, num_segments=num_nodes)
            return out + b

        def leaky(x):
            return jnp.where(x >= 0, x, RRELU_SLOPE * x)
        key = jax.random.key(seed)
        ks = jax.random.split(key, 8)
        x = jax.random.normal(ks[0], (N_NODES, IN_FEATS), dtype=jnp.float32)
        edge_index = jax.random.randint(ks[1], (2, N_EDGES), 0, N_NODES, dtype=jnp.int64)

        def glorot(k, shape):
            lim = (6.0 / (shape[0] + shape[1])) ** 0.5
            return jax.random.uniform(k, shape, jnp.float32, -lim, lim)
        W1 = glorot(ks[2], (IN_FEATS, HIDDEN))
        b1 = jnp.zeros((HIDDEN,), jnp.float32)
        W2 = glorot(ks[3], (HIDDEN, HIDDEN))
        b2 = jnp.zeros((HIDDEN,), jnp.float32)
        Wl = glorot(ks[4], (HIDDEN, OUT_FEATS))
        bl = jax.random.uniform(ks[5], (OUT_FEATS,), jnp.float32, -0.1, 0.1)
        return {'x': x, 'edge_index': edge_index, 'W1': W1, 'b1': b1, 'W2': W2, 'b2': b2, 'Wl': Wl, 'bl': bl}
    _L1_gnn_all = _L1_gnn_setup()
    _L1_gnn_in = {k: v for k, v in _L1_gnn_all.items() if k in ('W1', 'b1', 'W2', 'b2', 'Wl', 'bl')}
    del _L1_gnn_all

    def _L2_gnn_setup():
        import jax, jax.numpy as jnp
        import numpy as np
        N_NODES = 12500
        N_EDGES = 200000
        IN_FEATS = 32
        OUT_FEATS = 32
        key = jax.random.key(seed)
        k1, k2, k3, k4, k5 = jax.random.split(key, 5)
        feature = jax.random.normal(k1, (N_NODES, IN_FEATS), dtype=jnp.float32)
        src = jax.random.randint(k2, (N_EDGES,), 0, N_NODES, dtype=jnp.int64)
        dst = jax.random.randint(k3, (N_EDGES,), 0, N_NODES, dtype=jnp.int64)
        dst = jnp.where(dst == src, (dst + 1) % N_NODES, dst)
        W = jax.random.normal(k4, (OUT_FEATS, IN_FEATS), dtype=jnp.float32) / np.sqrt(IN_FEATS)
        bias = jnp.zeros((OUT_FEATS,), dtype=jnp.float32)
        return {'feature': feature, 'src': src, 'dst': dst, 'W': W, 'bias': bias}
    _L2_gnn_all = _L2_gnn_setup()
    _L2_gnn_in = {k: v for k, v in _L2_gnn_all.items() if k in ('W', 'bias')}
    del _L2_gnn_all

    def _L3_gnn_setup():
        import jax, jax.numpy as jnp
        import numpy as np
        MUL = 16
        MOUT = 8
        TANH_GAIN = 1.593
        INV_SQRT3 = 0.5773502691896258
        PW_S = 0.17677669529663687
        PW_V = 0.25

        def _w3j_121():
            s2, s6 = (2 ** 0.5, 6 ** 0.5)
            M = np.zeros((5, 3, 3))
            M[0, 0, 1] = M[0, 1, 0] = 1 / s2
            M[1, 1, 2] = M[1, 2, 1] = 1 / s2
            M[2] = np.diag([-1.0, -1.0, 2.0]) / s6
            M[3, 0, 2] = M[3, 2, 0] = 1 / s2
            M[4] = np.diag([1.0, -1.0, 0.0]) / s2
            return jnp.asarray(np.transpose(M, (1, 0, 2)) / 5 ** 0.5, jnp.float32)
        W3J121 = _w3j_121()

        def _sph(edge_vec):
            n = edge_vec / jnp.linalg.norm(edge_vec, axis=1, keepdims=True)
            x, y, z = (n[:, 0], n[:, 1], n[:, 2])
            y1 = 3.0 ** 0.5 * n
            s15 = 15.0 ** 0.5
            y2 = jnp.stack([s15 * x * y, s15 * y * z, 5.0 ** 0.5 / 2 * (3 * z * z - 1), s15 * x * z, s15 / 2 * (x * x - y * y)], axis=1)
            return (y1, y2)

        def _forward(x, edge_src, edge_dst, edge_vec, emb, norm, W1, W2):
            N, E = (x.shape[0], edge_src.shape[0])
            xs = jnp.concatenate([x[edge_src, :8], x[edge_dst, :8]], axis=1)
            xv = jnp.concatenate([x[edge_src, 8:].reshape(E, 8, 3), x[edge_dst, 8:].reshape(E, 8, 3)], axis=1)
            y1, y2 = _sph(edge_vec)
            h = 2.0 ** 0.5 * jax.nn.relu(emb @ W1 / 10.0 ** 0.5)
            w = (h @ W2 / 16.0 ** 0.5).reshape(E, 7, MUL, MOUT)
            wa_s, wb_s, wa_g, wb_g, wc, wd, we = [w[:, i] for i in range(7)]
            s_out = PW_S * (jnp.einsum('eu,euw->ew', xs, wa_s) + INV_SQRT3 * jnp.einsum('eui,ei,euw->ew', xv, y1, wb_s))
            g_out = PW_S * (jnp.einsum('eu,euw->ew', xs, wa_g) + INV_SQRT3 * jnp.einsum('eui,ei,euw->ew', xv, y1, wb_g))
            v_out = PW_V * (INV_SQRT3 * jnp.einsum('eu,ek,euw->ewk', xs, y1, wc) + INV_SQRT3 * jnp.einsum('eui,euw->ewi', xv, wd) + jnp.einsum('eui,ea,iak,euw->ewk', xv, y2, W3J121, we))
            s_act = TANH_GAIN * jnp.tanh(s_out)
            gates = TANH_GAIN * jnp.tanh(g_out)
            edge_ftr = jnp.concatenate([s_act, (gates[:, :, None] * v_out).reshape(E, 24)], axis=1) * norm[:, None]
            return jax.ops.segment_sum(edge_ftr, edge_dst, num_segments=N)
        key = jax.random.key(seed)
        ks = jax.random.split(key, 8)
        N, E = (6250, 37500)
        return {'x': jax.random.normal(ks[0], (N, 32), jnp.float32), 'edge_src': jax.random.randint(ks[1], (E,), 0, N), 'edge_dst': jax.random.randint(ks[2], (E,), 0, N), 'edge_vec': jax.random.normal(ks[3], (E, 3), jnp.float32), 'emb': jax.random.uniform(ks[4], (E, 10), jnp.float32), 'norm': jax.random.uniform(ks[5], (E,), jnp.float32), 'W1': jax.random.normal(ks[6], (10, 16), jnp.float32), 'W2': jax.random.normal(ks[7], (16, 896), jnp.float32)}
    _L3_gnn_all = _L3_gnn_setup()
    _L3_gnn_in = {k: v for k, v in _L3_gnn_all.items() if k in ('W1', 'W2')}
    del _L3_gnn_all
    return {'x': x, 'src': src, 'dst': dst, 'edge_attr_10': edge_attr_10, 'edge_attr_3': edge_attr_3, 'edge_weight': edge_weight, 'L1_gnn_W1': _L1_gnn_in['W1'], 'L1_gnn_b1': _L1_gnn_in['b1'], 'L1_gnn_W2': _L1_gnn_in['W2'], 'L1_gnn_b2': _L1_gnn_in['b2'], 'L1_gnn_Wl': _L1_gnn_in['Wl'], 'L1_gnn_bl': _L1_gnn_in['bl'], 'L2_gnn_W': _L2_gnn_in['W'], 'L2_gnn_bias': _L2_gnn_in['bias'], 'L3_gnn_W1': _L3_gnn_in['W1'], 'L3_gnn_W2': _L3_gnn_in['W2']}

def reference(x, src, dst, edge_attr_10, edge_attr_3, edge_weight, L1_gnn_W1, L1_gnn_b1, L1_gnn_W2, L1_gnn_b2, L1_gnn_Wl, L1_gnn_bl, L2_gnn_W, L2_gnn_bias, L3_gnn_W1, L3_gnn_W2):
    import jax
    import jax.numpy as jnp

    def _L0_gnn_ref(node_feat, edge_attr, edge_index, num_nodes):
        import jax, jax.numpy as jnp
        import numpy as np
        src, dst = (edge_index[0], edge_index[1])
        messages = node_feat[src] * edge_attr[:, None]
        aggr = jax.ops.segment_sum(messages, dst, num_segments=num_nodes)
        return aggr + node_feat

    def _L1_gnn_ref(x, edge_index, W1, b1, W2, b2, Wl, bl):
        import jax, jax.numpy as jnp
        import numpy as np
        N_NODES = 6250
        N_EDGES = 200000
        IN_FEATS = 32
        HIDDEN = 48
        OUT_FEATS = 32
        RRELU_SLOPE = (1.0 / 8.0 + 1.0 / 3.0) / 2.0

        def gcn_conv(x, src, dst, W, b, num_nodes):
            loop = jnp.arange(num_nodes, dtype=src.dtype)
            s = jnp.concatenate([src, loop])
            d = jnp.concatenate([dst, loop])
            ew = jnp.ones(s.shape[0], dtype=x.dtype)
            deg = jax.ops.segment_sum(ew, d, num_segments=num_nodes)
            dinv = jnp.where(deg > 0, deg ** (-0.5), 0.0)
            norm = dinv[s] * ew * dinv[d]
            h = x @ W
            msg = h[s] * norm[:, None]
            out = jax.ops.segment_sum(msg, d, num_segments=num_nodes)
            return out + b

        def leaky(x):
            return jnp.where(x >= 0, x, RRELU_SLOPE * x)
        src, dst = (edge_index[0], edge_index[1])
        n = x.shape[0]
        h = leaky(gcn_conv(x, src, dst, W1, b1, n))
        h = leaky(gcn_conv(h, src, dst, W2, b2, n))
        return h @ Wl + bl

    def _L2_gnn_ref(feature, src, dst, W, bias):
        import jax, jax.numpy as jnp
        import numpy as np
        N_NODES = 12500
        N_EDGES = 200000
        IN_FEATS = 32
        OUT_FEATS = 32
        n = feature.shape[0]
        loops = jnp.arange(n, dtype=src.dtype)
        src_all = jnp.concatenate([src, loops])
        dst_all = jnp.concatenate([dst, loops])
        deg = jax.ops.segment_sum(jnp.ones_like(dst_all, dtype=feature.dtype), dst_all, num_segments=n)
        deg = jnp.maximum(deg, 1.0)[:, None]
        inv_sqrt_deg = jax.lax.rsqrt(deg)
        h = jnp.einsum('ni,oi->no', feature * inv_sqrt_deg, W)
        agg = jax.ops.segment_sum(h[src_all], dst_all, num_segments=n)
        out = jax.nn.relu(agg * inv_sqrt_deg + bias)
        return out

    def _L3_gnn_ref(x, edge_src, edge_dst, edge_vec, emb, norm, W1, W2):
        import jax, jax.numpy as jnp
        import numpy as np
        MUL = 16
        MOUT = 8
        TANH_GAIN = 1.593
        INV_SQRT3 = 0.5773502691896258
        PW_S = 0.17677669529663687
        PW_V = 0.25

        def _w3j_121():
            s2, s6 = (2 ** 0.5, 6 ** 0.5)
            M = np.zeros((5, 3, 3))
            M[0, 0, 1] = M[0, 1, 0] = 1 / s2
            M[1, 1, 2] = M[1, 2, 1] = 1 / s2
            M[2] = np.diag([-1.0, -1.0, 2.0]) / s6
            M[3, 0, 2] = M[3, 2, 0] = 1 / s2
            M[4] = np.diag([1.0, -1.0, 0.0]) / s2
            return jnp.asarray(np.transpose(M, (1, 0, 2)) / 5 ** 0.5, jnp.float32)
        W3J121 = _w3j_121()

        def _sph(edge_vec):
            n = edge_vec / jnp.linalg.norm(edge_vec, axis=1, keepdims=True)
            x, y, z = (n[:, 0], n[:, 1], n[:, 2])
            y1 = 3.0 ** 0.5 * n
            s15 = 15.0 ** 0.5
            y2 = jnp.stack([s15 * x * y, s15 * y * z, 5.0 ** 0.5 / 2 * (3 * z * z - 1), s15 * x * z, s15 / 2 * (x * x - y * y)], axis=1)
            return (y1, y2)

        def _forward(x, edge_src, edge_dst, edge_vec, emb, norm, W1, W2):
            N, E = (x.shape[0], edge_src.shape[0])
            xs = jnp.concatenate([x[edge_src, :8], x[edge_dst, :8]], axis=1)
            xv = jnp.concatenate([x[edge_src, 8:].reshape(E, 8, 3), x[edge_dst, 8:].reshape(E, 8, 3)], axis=1)
            y1, y2 = _sph(edge_vec)
            h = 2.0 ** 0.5 * jax.nn.relu(emb @ W1 / 10.0 ** 0.5)
            w = (h @ W2 / 16.0 ** 0.5).reshape(E, 7, MUL, MOUT)
            wa_s, wb_s, wa_g, wb_g, wc, wd, we = [w[:, i] for i in range(7)]
            s_out = PW_S * (jnp.einsum('eu,euw->ew', xs, wa_s) + INV_SQRT3 * jnp.einsum('eui,ei,euw->ew', xv, y1, wb_s))
            g_out = PW_S * (jnp.einsum('eu,euw->ew', xs, wa_g) + INV_SQRT3 * jnp.einsum('eui,ei,euw->ew', xv, y1, wb_g))
            v_out = PW_V * (INV_SQRT3 * jnp.einsum('eu,ek,euw->ewk', xs, y1, wc) + INV_SQRT3 * jnp.einsum('eui,euw->ewi', xv, wd) + jnp.einsum('eui,ea,iak,euw->ewk', xv, y2, W3J121, we))
            s_act = TANH_GAIN * jnp.tanh(s_out)
            gates = TANH_GAIN * jnp.tanh(g_out)
            edge_ftr = jnp.concatenate([s_act, (gates[:, :, None] * v_out).reshape(E, 24)], axis=1) * norm[:, None]
            return jax.ops.segment_sum(edge_ftr, edge_dst, num_segments=N)
        return _forward(x, edge_src, edge_dst, edge_vec, emb, norm, W1, W2)
    edge_index = jnp.stack([src, dst])
    x = _layernorm(x + _L0_gnn_ref(x, edge_weight, edge_index, 12500), axis=-1)
    x = _layernorm(x + _L1_gnn_ref(x, edge_index, L1_gnn_W1, L1_gnn_b1, L1_gnn_W2, L1_gnn_b2, L1_gnn_Wl, L1_gnn_bl), axis=-1)
    x = _layernorm(x + _L2_gnn_ref(x, src, dst, L2_gnn_W, L2_gnn_bias), axis=-1)
    x = _layernorm(x + _L3_gnn_ref(x, src, dst, edge_attr_3, edge_attr_10, edge_weight, L3_gnn_W1, L3_gnn_W2), axis=-1)
    return x

_drawn_inputs = setup_inputs


def setup_inputs(seed=0):
    import zlib

    import numpy as np

    out = dict(_drawn_inputs(seed))
    spreads = {'L1_gnn_b1': (0.0, 0.1), 'L1_gnn_b2': (0.0, 0.1), 'L2_gnn_bias': (0.0, 0.1)}
    factors = {}
    for name, (base, spread) in spreads.items():
        noise = np.random.default_rng([zlib.crc32(name.encode()), seed]).standard_normal(out[name].shape)
        drawn = base * np.exp(spread * noise) if base else spread * noise
        out[name] = jnp.asarray(drawn.astype(out[name].dtype))
    for name, factor in factors.items():
        out[name] = (out[name] * factor).astype(out[name].dtype)
    return out
```

```python
import numpy as np
import concourse.bass as bass
from concourse import mybir

F32 = mybir.dt.float32
BF16 = mybir.dt.bfloat16
I32 = mybir.dt.int32
ALU = mybir.AluOpType
ACT = mybir.ActivationFunctionType
AX = mybir.AxisListType

P = 128
N, E, D, H = 12500, 200000, 32, 48
NT = -(-N // P)
NP = NT * P
T = 1568
EP = T * P
C = 28
NIT = T // C // 2
C3 = 14
NIT3 = T // C3 // 2
B3 = 7
NB = 14
NBLK = NT // NB
QE = 4 * P
RAD = 16
MUL, MOUT = 16, 8
WA, WB, WF = MUL * 24, MUL * 24, MUL * 8
SLOPE = (1.0 / 8.0 + 1.0 / 3.0) / 2.0
EPS = 1e-5
STOP = 4
PW_S, PW_V, INV_SQRT3, TANH_GAIN = 0.17677669529663687, 0.25, 0.5773502691896258, 1.593
RADIAL_SCALE = 2.0 ** 0.5 / 10.0 ** 0.5 / 16.0 ** 0.5
BIG = 3 * P + P + 4 + NT


class Chain:

    def __init__(self, eng, sem):
        self.eng, self.sem, self.base, self.k = eng, sem, 0, 0

    def inc(self, ins):
        ins.then_inc(self.sem, 1)
        self.k += 1

    def sync(self):
        self.eng.wait_ge(self.sem, self.base + self.k)

    def enter(self, i, per):
        self.start, self.per = self.k, per
        self.base, self.k = i * per + self.start, 0

    def leave(self, turns):
        assert self.k == self.per, (self.k, self.per)
        self.base, self.k = 0, self.start + turns * self.per


def bc(ap, axis, n):
    v = ap.unsqueeze(axis)
    shape = list(v.shape)
    shape[axis] = n
    return v.to_broadcast(shape)


def gnn(nc, x_in, src, dst, ea10, ea3, ew, W1, b1, W2, b2, Wl, bl, W3T, b3, R1, R2, cst, out, stop=4):
    from contextlib import ExitStack
    ctx = ExitStack()
    with ctx:
        def sb(name, shape, dt=F32):
            return ctx.enter_context(nc.sbuf_tensor(name, shape, dt))

        def ps(name, shape):
            return ctx.enter_context(nc.psum_tensor(name, shape, F32))

        def sem(name):
            return ctx.enter_context(nc.semaphore(name))

        def dram(name, shape, dt=F32):
            return nc.dram_tensor(name, shape, dt, kind="Internal").ap()

        tables = [x_in, dram("tab1", [NP, D]), dram("tab2", [NP, H]), dram("tab3", [NP, D]), dram("tab4", [NP, D])]
        width = [D, D, H, D, D]
        sums = [dram(f"sums{k}", [EP, width[k]]) for k in range(5)]
        radial_d = dram("radial", [P, T * P], BF16)

        cs = sb("cs", [P, BIG])
        ident, tri, before, iota = (cs[:, k * P:(k + 1) * P] for k in range(4))
        rows_of = [cs[:, 4 * P + k:4 * P + k + 1] for k in range(3)]
        edge0 = cs[:, 4 * P + 3:4 * P + 4]
        iota_b = sb("iota_b", [P, P], BF16)
        zero_b = sb("zero_b", [P, P], BF16)
        ones = sb("ones", [P, P])
        mask = sb("mask", [P, T])
        wgt = sb("wgt", [P, T])
        unit = sb("unit", [P, T * 3])
        big = sb("big", [P, 14080])
        grows = sb("grows", [P, 2 * C * H])
        idx = sb("idx", [P, 4 * C], I32)
        xs = sb("xs", [P, NT * D])
        own = sb("own", [P, NT * H])
        agg = sb("agg", [P, NT * H])
        carry = sb("carry", [P, H])
        fix = sb("fix", [P, H])
        same = sb("same", [P, P])
        firstd = sb("firstd", [P, 1])
        lastd = sb("lastd", [P, 1])
        ends = sb("ends", [P, NT], I32)
        end1 = sb("end1", [P, 1], I32)
        stat = sb("stat", [P, 8 * NT])
        posm = sb("posm", [P, NT])
        dinv = sb("dinv", [P, NT])
        blk1 = sb("blk1", [64, 96])
        blk2 = sb("blk2", [96, 96])
        blkl = sb("blkl", [96, 64])
        blk3 = sb("blk3", [64, 64])
        bias = sb("bias", [P, 2 * H + 2 * D])
        bias1, bias2 = bias[:, 0:H], bias[:, H:2 * H]
        biasl, bias3 = bias[:, 2 * H:2 * H + D], bias[:, 2 * H + D:]
        rw1 = sb("rw1", [10, P])
        rw1s = sb("rw1s", [10, RAD])
        wsp = sb("wsp", [P, 896], BF16)

        dstf = big[:, 0:T]
        dsti = big[:, T:2 * T].bitcast(I32)
        tmpi = big[:, 2 * T:3 * T].bitcast(I32)
        b_lo = big[:, 2 * T + T:3 * T + T // 2].bitcast(BF16)
        b_hi = big[:, 3 * T + T // 2:4 * T].bitcast(BF16)
        o = 4 * T
        onelo = [big[:, o + h * C * P // 2:o + (h + 1) * C * P // 2].bitcast(BF16) for h in range(2)]
        o += C * P
        onehi = [big[:, o + h * C * NT // 2:o + (h + 1) * C * NT // 2].bitcast(BF16) for h in range(2)]
        nrm = agg[:, 0:T]
        nrm2 = agg[:, T:2 * T]
        sq3 = own[:, 0:T * 3]
        w8 = big[:, 4 * T:4 * T + 896]
        wc = big[:, 4 * T + 896:4 * T + 1792]
        wb1 = big[:, 4 * T + 1792:4 * T + 2240].bitcast(BF16)
        wb2 = big[:, 4 * T + 2240:4 * T + 2688].bitcast(BF16)
        QC = C // 4
        emb = [big[0:10, h * QC * QE:(h + 1) * QC * QE] for h in range(2)]
        hres = [big[:, 2 * QC * QE + k * QE:2 * QC * QE + (k + 1) * QE] for k in range(2)]
        o = 2 * QC * QE + 2 * QE
        hspl = [big[:, o + h * QC * QE // 2:o + (h + 1) * QC * QE // 2].bitcast(BF16) for h in range(2)]
        o += QC * QE
        hmid = big[:, o:o + QE // 2].bitcast(BF16)
        stage_in = big[:, 0:NB * H]
        stage_T = big[:, 1024:1024 + 7 * P]
        work = big[:, 2048:2048 + NT * D]
        own48 = big[:, 5248:5248 + NT * H]
        rad = [big[:, h * C3 * P // 2:(h + 1) * C3 * P // 2].bitcast(BF16) for h in range(2)]
        o = C3 * P
        prod = [big[:, o + k * MUL * 72:o + (k + 1) * MUL * 72] for k in range(2)]
        o += 2 * MUL * 72
        xsc = [big[:, o + h * C3 * 64:o + h * C3 * 64 + C3 * 16] for h in range(2)]
        xve = [big[:, o + h * C3 * 64 + C3 * 16:o + (h + 1) * C3 * 64] for h in range(2)]
        o += 2 * C3 * 64
        pm = big[:, o:o + C3 * 48]
        o += C3 * 48
        pr = [big[:, o + h * C3 * 16:o + (h + 1) * C3 * 16] for h in range(2)]
        o += 2 * C3 * 16
        red = [big[:, o + k * B3 * 72:o + (k + 1) * B3 * 72] for k in range(2)]
        o += 2 * B3 * 72
        sc = [big[:, o + k * B3 * 24:o + (k + 1) * B3 * 24] for k in range(2)]
        o += 2 * B3 * 24
        th = [big[:, o + k * B3 * 16:o + (k + 1) * B3 * 16] for k in range(2)]
        o += 2 * B3 * 16
        vec = [big[:, o + k * B3 * 24:o + (k + 1) * B3 * 24] for k in range(2)]
        o += 2 * B3 * 24
        msg = [big[:, o + h * C3 * D:o + (h + 1) * C3 * D] for h in range(2)]
        o += 2 * C3 * D
        assert o <= 14080, o

        bank = [ps(f"bank{k}", [P, 512]) for k in range(8)]
        hist = bank[0][:, 0:NT]

        s_cst, s_small, s_dst, s_ea, s_w8, s_x, s_bias = (sem(n) for n in (
            "s_cst", "s_small", "s_dst", "s_ea", "s_w8", "s_x", "s_bias"))
        s_v = sem("vector_chain")
        s_blk0, s_blk = sem("blocks_zeroed"), sem("blocks_loaded")
        s_sq, s_root = sem("square_ready"), sem("root_ready")
        s_setup = sem("setup_done")
        s_idx = [[sem(f"idx_in{k}{h}") for h in range(2)] for k in range(5)]
        s_g = [[sem(f"rows_in{k}{h}") for h in range(2)] for k in range(5)]
        s_scan = [sem(f"scanned{k}") for k in range(5)]
        s_st = [[sem(f"sums_out{k}{h}") for h in range(2)] for k in range(5)]
        s_tab = sem("table_out")
        s_fixmm, s_fixin, s_fixsum, s_fixout, s_node = (sem(n) for n in (
            "carry_summed", "fix_rows_in", "fix_added", "fix_rows_out", "node_rows_in"))
        s_ends = sem("ends_ready")
        s_one, s_hist, s_h0 = sem("onehot_ready"), sem("hist_done"), sem("hist_first")
        s_cum, s_cumd = sem("counts_ready"), sem("prefix_done")
        s_same, s_samed = sem("diag_ready"), sem("diag_done")
        s_stage, s_tp, s_tc, s_mm = sem("stage_in"), sem("transposed"), sem("transposed_copied"), sem("stage_mm")
        s_emb = [sem("emb_in0"), sem("emb_in1")]
        s_hmm, s_hact, s_hdone, s_hout = sem("h_mm"), sem("h_act"), sem("h_split"), [sem("h_out0"), sem("h_out1")]
        s_tabrdy = sem("table_ready")
        s_out = sem("out")
        s_rad = [sem("rad_in0"), sem("rad_in1")]
        s_wmm, s_mul, s_red, s_redc, s_sc, s_th = sem("w_mm"), sem("products"), sem("reduced"), sem("reduced_copied"), sem("scalars"), sem("tanh_ready")
        s_xc = sem("x_compact")
        s_gate = {e: sem(f"gate_{e}") for e in ("pool", "sp", "act", "pe", "dve")}

        def gate(eng, who, s, v):
            eng.wait_ge(s, v)
            eng.sem_inc(s_gate[who], 1)

        stores = 0
        block = ctx.enter_context(nc.Block())

        def rows(ap, k):
            return ap.rearrange("p (t f) -> p t f", f=k)

        sums_v = [s.rearrange("(p t) f -> p (t f)", p=P) for s in sums]
        npass = min(5, stop + 1) if stop > 1 else stop
        passes = list(range({1: 1, 2: 3, 3: 4, 4: 5}[stop]))

        @block.sync
        def _(sp):
            sp.dma_start(cs[:, :], cst).then_inc(s_cst, 16)
            sp.dma_start(dsti, dst).then_inc(s_dst, 16)
            sp.dma_start(wgt[:, :], ew).then_inc(s_ea, 16)
            sp.dma_start(unit[:, :], ea3).then_inc(s_ea, 16)
            for g in range(8):
                sp.dma_start(w8[g * RAD:(g + 1) * RAD, :], R2).then_inc(s_w8, 16)
            sp.dma_start(rw1s[:, :], R1).then_inc(s_small, 16)
            sp.dma_start(rows(xs[:, :], D), x_in.rearrange("(j p) f -> p j f", p=P)).then_inc(s_x, 16)
            for b, s in ((b1, bias1), (b2, bias2), (bl, biasl), (b3, bias3)):
                sp.dma_start(s, b.to_broadcast([P, b.shape[1]])).then_inc(s_bias, 16)
            sp.wait_ge(s_blk0, 1)
            for m, W, fi, fo in ((blk1, W1, D, H), (blk2, W2, H, H), (blkl, Wl, H, D), (blk3, W3T, D, D)):
                for q in range(2):
                    sp.dma_start(m[q * fi:(q + 1) * fi, q * fo:(q + 1) * fo], W).then_inc(s_blk, 16)

            def pass_traffic(k, f):
                src_v = src
                half = C * f
                for h in range(2):
                    sp.dma_start(idx[:, h * C:(h + 1) * C], src_v[:, h * C:(h + 1) * C]).then_inc(s_idx[k][h], 16)

                def turn(i, last):
                    for h in range(2):
                        gate(sp, "sp", s_scan[k], 2 * i + h + 1)
                        sp.dma_start(sums_v[k][:, bass.ds((2 * i + h) * half, half)],
                                     grows[:, h * half:(h + 1) * half]).then_inc(s_st[k][h], 16)
                        if not last:
                            sp.dma_start(idx[:, h * C:(h + 1) * C],
                                         src_v[:, bass.ds((2 * i + 2 + h) * C, C)]).then_inc(s_idx[k][h], 16)
                        if k == 1:
                            gate(sp, "sp", s_hdone, QC * (2 * i + h + 1))
                            sp.dma_start(radial_d[:, bass.ds((2 * i + h) * (C * P), C * P)], hspl[h]).then_inc(s_hout[h], 16)
                            if not last:
                                sp.dma_start(emb[h], ea10[:, bass.ds((2 * i + 2 + h) * (C * P), C * P)]).then_inc(s_emb[h], 16)

                if k == 1:
                    for h in range(2):
                        sp.dma_start(emb[h], ea10[:, h * C * P:(h + 1) * C * P]).then_inc(s_emb[h], 16)
                with sp.Fori(0, NIT - 1) as i:
                    turn(i, False)
                turn(NIT - 1, True)

            def table_out(k, n):
                sp.wait_ge(s_tabrdy, n)
                f = width[k]
                a = xs if k == 4 else own
                sp.dma_start(tables[k].rearrange("(j p) f -> p j f", p=P), rows(a[:, 0:NT * f], f)).then_inc(s_tab, 16)

            n = 0
            for k in passes:
                if k == 4:
                    msg_traffic = True
                    for h in range(2):
                        for q, ind in enumerate((src, dst)):
                            sp.dma_start(idx[:, (2 * h + q) * C3:(2 * h + q + 1) * C3],
                                         ind[:, h * C3:(h + 1) * C3]).then_inc(s_idx[k][h], 16)
                        sp.dma_start(rad[h], radial_d[:, h * C3 * P:(h + 1) * C3 * P]).then_inc(s_rad[h], 16)

                    def turn(i, last):
                        for h in range(2):
                            gate(sp, "sp", s_scan[4], 2 * i + h + 1)
                            sp.dma_start(sums_v[4][:, bass.ds((2 * i + h) * (C3 * D), C3 * D)], msg[h]).then_inc(s_st[4][h], 16)
                            if not last:
                                for q, ind in enumerate((src, dst)):
                                    sp.dma_start(idx[:, (2 * h + q) * C3:(2 * h + q + 1) * C3],
                                                 ind[:, bass.ds((2 * i + 2 + h) * C3, C3)]).then_inc(s_idx[4][h], 16)
                                sp.dma_start(rad[h], radial_d[:, bass.ds((2 * i + 2 + h) * (C3 * P), C3 * P)]).then_inc(s_rad[h], 16)
                    with sp.Fori(0, NIT3 - 1) as i:
                        turn(i, False)
                    turn(NIT3 - 1, True)
                else:
                    pass_traffic(k, width[k])
                if k + 1 in passes:
                    table_out(k + 1, k + 1)
            sp.wait_ge(s_tabrdy, len(passes))
            sp.dma_start(out.rearrange("(j p) f -> p j f", p=P), rows(xs[:, :], D)).then_inc(s_out, 16)
            sp.wait_ge(s_out, 16)

        @block.gpsimd
        def _(pool):
            for k in passes:
                f = width[k]
                if k:
                    pool.wait_ge(s_tab, 16 * k)
                if k < 4:
                    def turn(i, first):
                        for h in range(2):
                            gate(pool, "pool", s_idx[k][h], 16 * i + 16)
                            if not first:
                                gate(pool, "pool", s_st[k][h], 16 * i)
                            for j in range(C):
                                pool.indirect_dma_start(
                                    grows[:, (h * C + j) * f:(h * C + j + 1) * f], None, tables[k],
                                    bass.IndirectOffsetOnAxis(idx[:, h * C + j:h * C + j + 1], 0)).then_inc(s_g[k][h], 16)
                    turn(0, True)
                    with pool.Fori(1, NIT) as i:
                        turn(i, False)
                    turns = NIT
                else:
                    def turn(i, first):
                        for h in range(2):
                            gate(pool, "pool", s_idx[4][h], 32 * i + 32)
                            if not first:
                                gate(pool, "pool", s_xc, 2 * i + h - 1)
                            for j in range(C3):
                                for q in range(2):
                                    at = ((h * C3 + j) * 2 + q)
                                    pool.indirect_dma_start(
                                        grows[:, at * D:(at + 1) * D], None, tables[4],
                                        bass.IndirectOffsetOnAxis(idx[:, (2 * h + q) * C3 + j:(2 * h + q) * C3 + j + 1], 0)
                                    ).then_inc(s_g[4][h], 16)
                    turn(0, True)
                    with pool.Fori(1, NIT3) as i:
                        turn(i, False)
                    turns = NIT3
                for h in range(2):
                    pool.wait_ge(s_st[k][h], 16 * turns)
                if k == 0:
                    pool.wait_ge(s_ends, 1)
                pool.indirect_dma_start(fix[:, 0:f], None, sums[k], bass.IndirectOffsetOnAxis(end1[:, 0:1], 0)).then_inc(s_fixin, 16)
                pool.wait_ge(s_fixsum, k + 1)
                pool.indirect_dma_start(sums[k], bass.IndirectOffsetOnAxis(end1[:, 0:1], 0), fix[:, 0:f], None).then_inc(s_fixout, 16)
                pool.wait_ge(s_fixout, 16 * (k + 1))
                if k == 0:
                    pool.wait_ge(s_ends, 2)
                for j in range(NT):
                    pool.indirect_dma_start(agg[:, j * f:(j + 1) * f], None, sums[k],
                                            bass.IndirectOffsetOnAxis(ends[:, j:j + 1], 0)).then_inc(s_node, 16)

        @block.scalar
        def _(act):
            act.wait_ge(s_sq, 1)
            act.activation(nrm, nrm, ACT.Sqrt).then_inc(s_root, 1)
            roots = 1

            for k in passes:
                if k == 0:
                    act.wait_ge(s_sq, roots + 1)
                    act.activation(stat[:, NT:2 * NT], stat[:, 0:NT], ACT.Sqrt).then_inc(s_root, 1)
                    roots += 1
                if k == 1:
                    def turn(i, first):
                        for h in range(2):
                            if not first:
                                gate(act, "act", s_hout[h], 16 * i)
                            for q in range(QC):
                                n = (2 * i + h) * QC + q
                                gate(act, "act", s_hmm, n + 1)
                                pb = bank[2 + (h * QC + q) % 2][:, :]
                                act.activation(hspl[h][:, q * QE:(q + 1) * QE], pb, ACT.Relu, scale=RADIAL_SCALE).then_inc(s_hact, 1)
                                if not (first and h == 0 and q < 2):
                                    gate(act, "act", s_hdone, n - 1)
                                act.activation(hres[(h * QC + q) % 2], pb, ACT.Relu, scale=RADIAL_SCALE).then_inc(s_hact, 1)
                    turn(0, True)
                    with act.Fori(1, NIT) as i:
                        turn(i, False)
                if k == 4:
                    def turn(i, first):
                        for h in range(2):
                            gate(act, "act", s_g[4][h], 16 * 2 * C3 * (i + 1))
                            if not first:
                                gate(act, "act", s_scan[4], 2 * i + h - 1)
                            g = rows(grows[:, h * C3 * 64:(h + 1) * C3 * 64], D)
                            act.copy(rows(xsc[h], 8), g[:, :, 0:8])
                            act.copy(rows(xve[h], 24), g[:, :, 8:32]).then_inc(s_xc, 1)
                            for b in range(2):
                                n = (2 * i + h) * 2 + b
                                gate(act, "act", s_red, B3 * (n + 1))
                                if not (first and h == 0):
                                    gate(act, "act", s_sc, 2 * (n - 1))
                                act.copy(red[b], bank[4 + b][:, 0:B3 * 72]).then_inc(s_redc, 1)
                                gate(act, "act", s_sc, 2 * n + 1)
                                act.activation(rows(th[b], 16), rows(sc[b], 24)[:, :, 0:16], ACT.Tanh).then_inc(s_th, 1)
                    turn(0, True)
                    with act.Fori(1, NIT3) as i:
                        turn(i, False)
                for st in {0: [], 1: [0], 2: [1, 2], 3: [3], 4: []}[k]:
                    fi = (D, H, H, D)[st]
                    with act.Fori(0, NBLK) as b:
                        gate(act, "act", s_tp, st * NBLK + b + 1)
                        act.copy(stage_T[0:2 * fi, 0:4 * P], bank[0][0:2 * fi, :])
                        act.copy(stage_T[0:2 * fi, 4 * P:7 * P], bank[1][0:2 * fi, 0:3 * P]).then_inc(s_tc, 1)
                if k != 1:
                    act.wait_ge(s_sq, roots + 1)
                    act.activation(stat[:, NT:2 * NT], stat[:, 0:NT], ACT.Sqrt).then_inc(s_root, 1)
                    roots += 1

        @block.vector
        def _(v):
            ch = Chain(v, s_v)
            TT, TS = v.tensor_tensor, v.tensor_scalar

            def step(ins):
                ch.inc(ins)
                ch.sync()

            for m in (blk1, blk2, blkl, blk3):
                last = v.memset(m[:, :], 0.0)
            ch.inc(last)
            ch.sync()
            v.sem_inc(s_blk0, 1)
            v.wait_ge(s_cst, 16)
            v.wait_ge(s_dst, 16)
            step(v.tensor_copy(dstf, dsti))
            v.tensor_copy(iota_b[:, :], iota)
            v.memset(mask[:, 0:1], 0.0)
            v.tensor_copy(firstd[:, :], dstf[:, 0:1])
            v.tensor_copy(lastd[:, :], dstf[:, T - 1:T])
            TT(mask[:, 1:T], dstf[:, 1:T], dstf[:, 0:T - 1], ALU.is_equal)
            step(v.tensor_single_scalar(tmpi, dsti, 7, ALU.logical_shift_right))
            step(v.tensor_copy(b_hi, tmpi))
            step(v.tensor_single_scalar(tmpi, dsti, 127, ALU.bitwise_and))
            step(v.tensor_copy(b_lo, tmpi))
            step(TS(agg[:, 0:T], dstf, firstd[:, 0:1], None, ALU.is_equal))
            step(v.tensor_reduce(stat[:, 0:1], agg[:, 0:T], axis=AX.X, op=ALU.add))
            step(TS(stat[:, 1:2], stat[:, 0:1], edge0, -1.0, ALU.add, ALU.add))
            v.tensor_copy(end1[:, :], stat[:, 1:2])
            step(TS(same[:, :], ident, firstd[:, 0:1], None, ALU.mult))
            v.memset(ones[:, :], 1.0).then_inc(s_same, 1)
            v.wait_ge(s_samed, 1)
            step(TS(same[:, :], bank[1][:, 0:P], lastd[:, 0:1], None, ALU.is_equal))
            TT(same[:, :], same[:, :], before, ALU.mult).then_inc(s_ends, 1)
            v.wait_ge(s_ea, 32)
            step(TT(sq3, unit[:, :], unit[:, :], ALU.mult))
            v.tensor_reduce(nrm2, rows(sq3, 3), axis=AX.X, op=ALU.add)
            v.tensor_reduce(nrm, rows(sq3, 3), axis=AX.X, op=ALU.add).then_inc(s_sq, 1)

            def refine(y, d, t):
                step(v.reciprocal(y, y))
                step(TT(t, y, y, ALU.mult))
                step(TT(t, t, d, ALU.mult))
                step(TS(t, t, -0.5, 1.5, ALU.mult, ALU.add))
                step(TT(y, y, t, ALU.mult))

            v.wait_ge(s_w8, 128)
            wv = w8.rearrange("p (k u w) -> p k u w", k=7, u=MUL)
            ab = wc[:, 0:WA].rearrange("p (u c) -> p u c", c=24)
            pb_ = wc[:, WA:WA + WB].rearrange("p (u c) -> p u c", c=24)
            fv = wc[:, WA + WB:896].rearrange("p (u c) -> p u c", c=8)
            for blk, dest, at, scale in ((0, ab, 0, PW_S), (2, ab, 8, PW_S), (4, ab, 16, PW_V),
                                         (1, pb_, 0, PW_S), (3, pb_, 8, PW_S), (6, pb_, 16, PW_V * 1.5 ** 0.5)):
                TS(dest[:, :, at:at + 8], wv[:, blk, :, :], scale, None, ALU.mult)
            step(TS(fv, wv[:, 6, :, :], -PW_V * 1.5 ** 0.5 / 3.0, None, ALU.mult))
            step(v.scalar_tensor_tensor(out=fv, in0=wv[:, 5, :, :], scalar=PW_V * INV_SQRT3, in1=fv, op0=ALU.mult, op1=ALU.add))
            step(v.tensor_copy(wb1, wc))
            step(TT(wc, wc, wb1, ALU.subtract))
            step(v.tensor_copy(wb2, wc))
            step(TT(wc, wc, wb2, ALU.subtract))
            step(TS(wsp[:, :], wc, rows_of[2], None, ALU.mult))
            step(v.scalar_tensor_tensor(out=wsp[:, :], in0=wb2, scalar=rows_of[1], in1=wsp[:, :], op0=ALU.mult, op1=ALU.add))
            step(v.scalar_tensor_tensor(out=wsp[:, :], in0=wb1, scalar=rows_of[0], in1=wsp[:, :], op0=ALU.mult, op1=ALU.add))
            v.wait_ge(s_small, 16)
            step(v.tensor_copy(rw1[:, :].rearrange("k (g r) -> k g r", g=8), bc(rw1s[:, :], 1, 8)))
            v.wait_ge(s_root, 1)
            refine(nrm, nrm2, own[:, 0:T])
            step(TT(rows(unit[:, :], 3), rows(unit[:, :], 3), bc(nrm, 2, 3), ALU.mult))
            v.memset(zero_b[:, :], 0.0).then_inc(s_h0, 1)
            roots = 1

            def scans(k, f, rowsbuf, i, h, cols):
                m = mask[:, bass.ds((2 * i + h) * cols, cols)]
                for c in range(f):
                    last = v.tensor_tensor_scan(out=rowsbuf[:, :, c], data0=m, data1=rowsbuf[:, :, c],
                                                initial=carry[:, c:c + 1], op0=ALU.mult, op1=ALU.add)
                step(last)
                step(v.tensor_copy(carry[:, 0:f], rowsbuf[:, cols - 1, :]))
                v.sem_inc(s_scan[k], 1)

            def newton_norm(x):
                nonlocal roots
                x3, w3 = rows(x, D), rows(work, D)
                s0, s1, s2, s3 = (stat[:, q * NT:(q + 1) * NT] for q in range(4))
                step(v.tensor_reduce(s2, x3, axis=AX.X, op=ALU.add))
                step(TS(s2, s2, 1.0 / D, None, ALU.mult))
                step(TT(x3, x3, bc(s2, 2, D), ALU.subtract))
                step(TT(work, x, x, ALU.mult))
                step(v.tensor_reduce(s2, w3, axis=AX.X, op=ALU.add))
                TS(s0, s2, 1.0 / D, EPS, ALU.mult, ALU.add).then_inc(s_sq, 1)
                roots += 1
                v.wait_ge(s_root, roots)
                refine(s1, s0, s3)
                step(TT(x3, x3, bc(s1, 2, D), ALU.mult))

            for k in passes:
                f = width[k]
                step(v.memset(carry[:, :], 0.0))
                if k < 4:
                    half = C * f

                    def body(i, h):
                        g = rows(grows[:, h * half:(h + 1) * half], f)
                        v.wait_ge(s_g[k][h], 16 * C * (i + 1))
                        if k == 0:
                            step(TT(g, g, bc(wgt[:, bass.ds((2 * i + h) * C, C)], 2, f), ALU.mult))
                        else:
                            v.sem_inc(s_gate["dve"], 1)
                        scans(k, f, g, i, h, C)
                        if k == 0:
                            gate(v, "dve", s_hist, 2 * i + 1)
                            lo = b_lo[:, bass.ds((2 * i + h) * C, C)]
                            hi = b_hi[:, bass.ds((2 * i + h) * C, C)]
                            TT(onelo[h].rearrange("p (t c) -> p t c", c=P), bc(lo, 2, P), bc(iota_b[:, :], 1, C), ALU.is_equal)
                            TT(onehi[h].rearrange("p (t c) -> p t c", c=NT), bc(hi, 2, NT), bc(iota_b[:, 0:NT], 1, C), ALU.is_equal).then_inc(s_one, 1)
                        if k == 1:
                            for q in range(QC):
                                n = (2 * i + h) * QC + q
                                hs = hspl[h][:, q * QE:(q + 1) * QE]
                                hr = hres[(h * QC + q) % 2]
                                v.wait_ge(s_hact, 2 * n + 2)
                                step(TT(hr, hr, hs, ALU.subtract))
                                step(v.tensor_copy(hmid, hr))
                                v.tensor_copy(hs[32:64, :], hmid[32:64, :])
                                TT(hs[96:128, :], hr[96:128, :], hmid[96:128, :], ALU.subtract).then_inc(s_hdone, 1)

                    per = {0: 6, 1: 2 * (2 + 2 * QC), 2: 4, 3: 4}[k]
                    with v.Fori(0, NIT) as i:
                        ch.enter(i, per)
                        for h in range(2):
                            body(i, h)
                    ch.leave(NIT)
                else:
                    def turn(i, first):
                        for h in range(2):
                            v.wait_ge(s_xc, 2 * i + h + 1)
                            xv4 = xve[h].rearrange("p (t u i) -> p t u i", u=MUL, i=3)
                            nv = unit[:, bass.ds((2 * i + h) * (C3 * 3), C3 * 3)].rearrange("p (t i) -> p t i", i=3)
                            pm4 = pm.rearrange("p (t u i) -> p t u i", u=MUL, i=3)
                            v.sem_inc(s_gate["dve"], 1)
                            for i3 in range(3):
                                last = TT(pm4[:, :, :, i3], xv4[:, :, :, i3], bc(nv[:, :, i3], 2, MUL), ALU.mult)
                            step(last)
                            step(v.tensor_reduce(rows(pr[h], MUL), pm4, axis=AX.X, op=ALU.add))
                            for b in range(2):
                                for j in range(B3):
                                    t = b * B3 + j
                                    n = (2 * i + h) * C3 + t
                                    q = (h * C3 + t) % 2
                                    pk = prod[q].rearrange("p (u c) -> p u c", c=72)
                                    v.wait_ge(s_wmm, n + 1)
                                    TT(pk[:, :, 0:24], bank[0 + q][:, 0:WA].rearrange("p (u c) -> p u c", c=24),
                                       bc(xsc[h][:, t * MUL:(t + 1) * MUL], 2, 24), ALU.mult)
                                    TT(pk[:, :, 24:48], bank[2 + q][:, 0:WB].rearrange("p (u c) -> p u c", c=24),
                                       bc(pr[h][:, t * MUL:(t + 1) * MUL], 2, 24), ALU.mult)
                                    TT(pk[:, :, 48:72].rearrange("p u (i w) -> p u i w", i=3),
                                       bc(bank[2 + q][:, WB:512].rearrange("p (u w) -> p u w", w=8), 2, 3),
                                       bc(xve[h][:, t * 48:(t + 1) * 48].rearrange("p (u i) -> p u i", i=3), 3, 8),
                                       ALU.mult).then_inc(s_mul, 1)
                                m = (2 * i + h) * 2 + b
                                r, s_, t_, e_ = rows(red[b], 72), rows(sc[b], 24), rows(th[b], 16), rows(vec[b], 24)
                                cols = bass.ds((2 * i + h) * C3 + b * B3, B3)
                                v.wait_ge(s_redc, m + 1)
                                TT(s_, r[:, :, 0:24], r[:, :, 24:48], ALU.add).then_inc(s_sc, 1)
                                v.wait_ge(s_th, m + 1)
                                step(TT(t_, t_, bc(wgt[:, cols], 2, 16), ALU.mult))
                                e4 = e_.rearrange("p t (i w) -> p t i w", i=3)
                                nb = unit[:, bass.ds(((2 * i + h) * C3 + b * B3) * 3, B3 * 3)].rearrange("p (t i) -> p t i", i=3)
                                for i3 in range(3):
                                    last = TT(e4[:, :, i3, :], s_[:, :, 16:24], bc(nb[:, :, i3], 2, 8), ALU.mult)
                                step(last)
                                step(TT(e_, e_, r[:, :, 48:72], ALU.add))
                                if b == 0 and not first:
                                    gate(v, "dve", s_st[4][h], 16 * i)
                                mg = rows(msg[h], D)[:, b * B3:(b + 1) * B3, :]
                                mv = mg[:, :, 8:32].rearrange("p t (w i) -> p t i w", i=3)
                                TS(mg[:, :, 0:8], t_[:, :, 0:8], TANH_GAIN, None, ALU.mult)
                                for i3 in range(3):
                                    last = v.scalar_tensor_tensor(out=mv[:, :, i3, :], in0=e4[:, :, i3, :], scalar=TANH_GAIN,
                                                           in1=t_[:, :, 8:16], op0=ALU.mult, op1=ALU.mult)
                                last.then_inc(s_sc, 1)
                            v.wait_ge(s_sc, 2 * (2 * (2 * i + h) + 2))
                            v.sem_inc(s_gate["dve"], 1)
                            scans(4, D, rows(msg[h], D), i, h, C3)
                    per = 2 * (2 + 2 * 3 + 2)
                    turn(0, True)
                    with v.Fori(1, NIT3) as i:
                        start = ch.k
                        ch.start, ch.per = start, per
                        ch.base, ch.k = (i - 1) * per + start, 0
                        turn(i, False)
                    ch.leave(NIT3 - 1)

                if k == 0:
                    v.wait_ge(s_hist, 2 * NIT + 2)
                    cnt = stat[:, 2 * NT:3 * NT]
                    step(v.tensor_copy(cnt, hist))
                    v.sem_inc(s_cum, 1)
                    step(TS(posm[:, :], cnt, 1.0, None, ALU.min))
                    TS(stat[:, 0:NT], cnt, 1.0, None, ALU.add).then_inc(s_sq, 1)
                    v.wait_ge(s_cumd, 1)
                    step(v.tensor_copy(stat[:, 3 * NT:4 * NT], bank[1][:, NT:2 * NT]))
                    step(v.memset(stat[:, 5 * NT:6 * NT], 1.0))
                    step(v.tensor_tensor_scan(out=stat[:, 4 * NT:5 * NT], data0=stat[:, 5 * NT:6 * NT], data1=stat[:, 3 * NT:4 * NT],
                                              initial=0.0, op0=ALU.mult, op1=ALU.add))
                    step(TT(stat[:, 4 * NT:5 * NT], stat[:, 4 * NT:5 * NT], stat[:, 3 * NT:4 * NT], ALU.subtract))
                    step(TT(stat[:, 4 * NT:5 * NT], stat[:, 4 * NT:5 * NT], bank[1][:, 0:NT], ALU.add))
                    step(TS(stat[:, 4 * NT:5 * NT], stat[:, 4 * NT:5 * NT], -1.0, 0.0, ALU.add, ALU.max))
                    v.tensor_copy(ends[:, :], stat[:, 4 * NT:5 * NT]).then_inc(s_ends, 1)
                    roots += 1
                    v.wait_ge(s_root, roots)
                    step(v.tensor_copy(dinv[:, :], stat[:, NT:2 * NT]))
                    refine(dinv[:, :], stat[:, 0:NT], stat[:, 5 * NT:6 * NT])
                v.wait_ge(s_fixin, 16 * (k + 1))
                v.wait_ge(s_fixmm, k + 1)
                TT(fix[:, 0:f], fix[:, 0:f], bank[7][:, 0:f], ALU.add).then_inc(s_fixsum, 1)
                v.wait_ge(s_node, 16 * NT * (k + 1))
                if k == 0:
                    v.wait_ge(s_x, 16)
                    v.wait_ge(s_bias, 64)
                a3 = rows(agg[:, 0:NT * f], f)
                o3 = rows(own[:, 0:NT * f], f)
                step(TT(a3, a3, bc(posm[:, :], 2, f), ALU.mult))
                if k == 0:
                    step(v.scalar_tensor_tensor(out=xs[:, :], in0=xs[:, :], scalar=2.0, in1=agg[:, 0:NT * D], op0=ALU.mult, op1=ALU.add))
                    newton_norm(xs[:, :])
                    step(TT(o3, rows(xs[:, :], D), bc(dinv[:, :], 2, D), ALU.mult))
                elif k < 4:
                    for st in {1: [0], 2: [1, 2], 3: [3]}[k]:
                        fi, fo = ((D, H), (H, H), (H, D), (D, D))[st]
                        per = {0: 6, 1: 5, 2: 3, 3: 6}[st]
                        with v.Fori(0, NBLK) as b:
                            ch.enter(b, per)
                            n = st * NBLK + b
                            si = rows(stage_in[:, 0:NB * fi], fi)
                            a = rows(agg[:, bass.ds(b * (NB * fi), NB * fi)], fi)
                            o_ = rows(own[:, bass.ds(b * (NB * fi), NB * fi)], fi)
                            dv = dinv[:, bass.ds(b * NB, NB)]
                            if st == 2:
                                ch.inc(v.tensor_copy(si, a))
                            else:
                                step(TT(si, a, o_, ALU.add))
                                ch.inc(TT(si, si, bc(dv, 2, fi), ALU.mult))
                            ch.sync()
                            v.sem_inc(s_stage, 1)
                            v.wait_ge(s_mm, n + 1)
                            v.sem_inc(s_gate["dve"], 1)
                            for part, (bk, c0, cn) in enumerate(((2, 0, 8), (3, 8, 6))):
                                pv = rows(bank[bk][:, 0:cn * fo], fo)
                                if st == 0 or st == 1:
                                    bb = bias1 if st == 0 else bias2
                                    w_ = rows(work[:, c0 * fo:(c0 + cn) * fo], fo)
                                    last = TT(w_, pv, bc(bb, 1, cn), ALU.add)
                                else:
                                    bb = biasl if st == 2 else bias3
                                    w_ = rows(work[:, c0 * fo:(c0 + cn) * fo], fo)
                                    last = TT(w_, pv, bc(bb, 1, cn), ALU.add)
                            step(last)
                            wk = work[:, 0:NB * fo]
                            if st in (0, 1):
                                dst_t = own48 if st == 0 else agg
                                dd = dst_t[:, bass.ds(b * (NB * fo), NB * fo)]
                                if st == 0:
                                    step(v.scalar_tensor_tensor(out=wk, in0=wk, scalar=SLOPE, in1=wk, op0=ALU.mult, op1=ALU.max))
                                    step(TT(rows(dd, fo), rows(wk, fo), bc(dv, 2, fo), ALU.mult))
                                    step(v.memset(stat[:, 7 * NT:7 * NT + 1], 0.0))
                                else:
                                    step(v.scalar_tensor_tensor(out=dd, in0=wk, scalar=SLOPE, in1=wk, op0=ALU.mult, op1=ALU.max))
                                    step(v.memset(stat[:, 7 * NT:7 * NT + 1], 0.0))
                            else:
                                xx = xs[:, bass.ds(b * (NB * fo), NB * fo)]
                                if st == 3:
                                    step(TS(wk, wk, 0.0, None, ALU.max))
                                    step(v.memset(stat[:, 7 * NT:7 * NT + 1], 0.0))
                                step(TT(xx, xx, wk, ALU.add))
                        ch.leave(NBLK)
                    if k == 1:
                        step(v.tensor_copy(own[:, :], own48))
                    if k >= 2:
                        newton_norm(xs[:, :])
                    if k == 2:
                        step(TT(rows(own[:, 0:NT * D], D), rows(xs[:, :], D), bc(dinv[:, :], 2, D), ALU.mult))
                else:
                    step(TT(xs[:, :], xs[:, :], agg[:, 0:NT * D], ALU.add))
                    newton_norm(xs[:, :])
                v.sem_inc(s_tabrdy, 1)

        @block.tensor
        def _(pe):
            pe.wait_ge(s_same, 1)
            pe.wait_ge(s_cst, 16)
            pe.matmul(bank[1][:, 0:P], ones[:, :], same[:, :], start=True, stop=True).then_inc(s_samed, 1)
            for k in passes:
                f = width[k]
                if k == 0:
                    pe.wait_ge(s_h0, 1)
                    pe.matmul(hist, zero_b[:, :], zero_b[:, 0:NT], start=True, stop=False).then_inc(s_hist, 1)
                    with pe.Fori(0, NIT) as i:
                        for h in range(2):
                            gate(pe, "pe", s_one, 2 * i + h + 1)
                            for j in range(C):
                                last = pe.matmul(hist, onelo[h][:, j * P:(j + 1) * P], onehi[h][:, j * NT:(j + 1) * NT],
                                                 start=False, stop=False)
                            last.then_inc(s_hist, 1)
                    pe.matmul(hist, zero_b[:, :], zero_b[:, 0:NT], start=False, stop=True).then_inc(s_hist, 1)
                    pe.wait_ge(s_cum, 1)
                    cnt = stat[:, 2 * NT:3 * NT]
                    pe.matmul(bank[1][:, 0:NT], tri, cnt, start=True, stop=True)
                    pe.matmul(bank[1][:, NT:2 * NT], ones[:, :], cnt, start=True, stop=True).then_inc(s_cumd, 1)
                if k == 1:
                    def turn(i, first):
                        for h in range(2):
                            gate(pe, "pe", s_emb[h], 16 * i + 16)
                            for q in range(QC):
                                n = (2 * i + h) * QC + q
                                if not (first and h == 0 and q < 2):
                                    gate(pe, "pe", s_hact, 2 * (n - 1))
                                pe.matmul(bank[2 + (h * QC + q) % 2][:, :], rw1[:, :], emb[h][:, q * QE:(q + 1) * QE],
                                          start=True, stop=True).then_inc(s_hmm, 1)
                    turn(0, True)
                    with pe.Fori(1, NIT) as i:
                        turn(i, False)
                if k == 4:
                    def turn(i, first):
                        def weights(h, t):
                            n = (2 * i + h) * C3 + t
                            q = (h * C3 + t) % 2
                            if t == 0:
                                gate(pe, "pe", s_rad[h], 16 * i + 16)
                            if not (first and h == 0 and t < 2):
                                gate(pe, "pe", s_mul, n - 1)
                            lt = rad[h][:, t * P:(t + 1) * P]
                            pe.matmul(bank[0 + q][:, 0:WA], lt, wsp[:, 0:WA], start=True, stop=True)
                            pe.matmul(bank[2 + q][:, :], lt, wsp[:, WA:896], start=True, stop=True).then_inc(s_wmm, 1)

                        def reduce(h, t):
                            n = (2 * i + h) * C3 + t
                            q = (h * C3 + t) % 2
                            b, j = t // B3, t % B3
                            gate(pe, "pe", s_mul, n + 1)
                            if j == 0 and not (first and h == 0):
                                gate(pe, "pe", s_redc, 2 * (2 * i + h) + b - 1)
                            for u in range(MUL):
                                last = pe.matmul(bank[4 + b][:, j * 72:(j + 1) * 72], ident, prod[q][:, u * 72:(u + 1) * 72],
                                                 start=(u == 0), stop=(u == MUL - 1))
                            last.then_inc(s_red, 1)

                        order = [(h, t) for h in range(2) for t in range(C3)]
                        weights(*order[0])
                        for a in range(1, len(order)):
                            weights(*order[a])
                            reduce(*order[a - 1])
                        reduce(*order[-1])
                    turn(0, True)
                    with pe.Fori(1, NIT3) as i:
                        turn(i, False)
                pe.wait_ge(s_scan[k], 2 * (NIT3 if k == 4 else NIT))
                pe.matmul(bank[7][:, 0:f], same[:, :], carry[:, 0:f], start=True, stop=True).then_inc(s_fixmm, 1)
                for st in {0: [], 1: [0], 2: [1, 2], 3: [3], 4: []}[k]:
                    fi, fo = ((D, H), (H, H), (H, D), (D, D))[st]
                    wb = (blk1, blk2, blkl, blk3)[st]
                    if st == 0:
                        pe.wait_ge(s_blk, 128)
                    with pe.Fori(0, NBLK) as b:
                        gate(pe, "pe", s_stage, st * NBLK + b + 1)
                        for q in range(7):
                            last = pe.transpose(bank[q // 4][0:2 * fi, (q % 4) * P:(q % 4 + 1) * P],
                                                stage_in[:, q * 2 * fi:(q + 1) * 2 * fi], ident)
                        last.then_inc(s_tp, 1)
                        gate(pe, "pe", s_tc, st * NBLK + b + 1)
                        for q in range(7):
                            last = pe.matmul(bank[2 + q // 4][:, (q % 4) * 2 * fo:(q % 4 + 1) * 2 * fo],
                                             stage_T[0:2 * fi, q * P:(q + 1) * P], wb[:, :], start=True, stop=True)
                        last.then_inc(s_mm, 1)


def kernel(x, src, dst, edge_attr_10, edge_attr_3, edge_weight, L1_gnn_W1, L1_gnn_b1, L1_gnn_W2, L1_gnn_b2,
           L1_gnn_Wl, L1_gnn_bl, L2_gnn_W, L2_gnn_bias, L3_gnn_W1, L3_gnn_W2):
    import numpy as _np
    import concourse.bacc as _bacc
    from concourse.bass_utils import run_bass_kernel_spmd as _run

    def edges(a, fill):
        a = _np.asarray(a)
        a = _np.concatenate([a, _np.full((EP - E,) + a.shape[1:], fill, a.dtype)])
        return a.reshape((P, T) + a.shape[1:])

    cst = _np.zeros((P, BIG), _np.float32)
    cst[:, 0:P] = _np.eye(P)
    cst[:, P:2 * P] = _np.triu(_np.ones((P, P)))
    cst[:, 2 * P:3 * P] = _np.triu(_np.ones((P, P)), 1)
    cst[:, 3 * P:4 * P] = _np.arange(P)
    parts = [0] * 16 + [1] * 16 + [0] * 16 + [1] * 16 + [2] * 16 + [-1] * 16 + [0] * 16 + [-1] * 16
    for k in range(3):
        cst[:, 4 * P + k] = _np.array([q == k for q in parts])
    cst[:, 4 * P + 3] = _np.arange(P) * T
    x = _np.asarray(x)
    arrays = {
        "x": _np.concatenate([x, _np.zeros((NP - N, D), x.dtype)]),
        "src": edges(src, 0), "dst": edges(dst, N),
        "ea10": _np.ascontiguousarray(edges(edge_attr_10, 0).transpose(2, 1, 0).reshape(10, T * P)),
        "ea3": edges(edge_attr_3, 1).reshape(P, T * 3), "ew": edges(edge_weight, 0),
        "W1": L1_gnn_W1, "b1": _np.asarray(L1_gnn_b1).reshape(1, H), "W2": L1_gnn_W2, "b2": _np.asarray(L1_gnn_b2).reshape(1, H),
        "Wl": L1_gnn_Wl, "bl": _np.asarray(L1_gnn_bl).reshape(1, D), "W3T": _np.ascontiguousarray(_np.asarray(L2_gnn_W).T),
        "b3": _np.asarray(L2_gnn_bias).reshape(1, D), "R1": L3_gnn_W1, "R2": L3_gnn_W2, "cst": cst,
    }
    arrays = {f"in_{n}": _np.ascontiguousarray(a) for n, a in arrays.items()}
    nc = _bacc.Bacc("TRN2", target_bir_lowering=False, num_devices=1)
    args = [nc.dram_tensor(n, a.shape, mybir.dt.from_np(a.dtype), kind="ExternalInput").ap() for n, a in arrays.items()]
    args.append(nc.dram_tensor("out_x", (NP, D), F32, kind="ExternalOutput").ap())
    gnn(nc, *args, stop=STOP)
    r = _run(nc, [arrays], core_ids=[0])
    return r.results[0]["out_x"][0:N]
```

```python
import numpy as np
import concourse.bass as bass
from concourse import mybir

F32 = mybir.dt.float32
BF16 = mybir.dt.bfloat16
I32 = mybir.dt.int32
ALU = mybir.AluOpType
ACT = mybir.ActivationFunctionType
AX = mybir.AxisListType

P = 128
N, E, D, H = 12500, 200000, 32, 48
NT = -(-N // P)
NP = NT * P
T = 1584
EP = T * P
C = 24
NIT = T // C // 2
C3 = 12
T3 = 2 * C3
NIT3 = T // T3
B3 = 6
NB = 14
NBLK = NT // NB
QE = 4 * P
RAD = 16
MUL, MOUT = 16, 8
WA, WB, WF = MUL * 24, MUL * 24, MUL * 8
SLOPE = (1.0 / 8.0 + 1.0 / 3.0) / 2.0
EPS = 1e-5
LAG = 2
TOKENS = 2
STOP = 4
PW_S, PW_V, INV_SQRT3, TANH_GAIN = 0.17677669529663687, 0.25, 0.5773502691896258, 1.593
RADIAL_SCALE = 2.0 ** 0.5 / 10.0 ** 0.5 / 16.0 ** 0.5
BIG = 3 * P + P + 4 + NT


class Chain:

    def __init__(self, eng, sem):
        self.eng, self.sem, self.base, self.k = eng, sem, 0, 0

    def inc(self, ins):
        ins.then_inc(self.sem, 1)
        self.k += 1

    def sync(self):
        self.eng.wait_ge(self.sem, self.base + self.k)

    def enter(self, i, per):
        self.start, self.per = self.k, per
        self.base, self.k = i * per + self.start, 0

    def leave(self, turns):
        assert self.k == self.per, (self.k, self.per)
        self.base, self.k = 0, self.start + turns * self.per


def bc(ap, axis, n):
    v = ap.unsqueeze(axis)
    shape = list(v.shape)
    shape[axis] = n
    return v.to_broadcast(shape)


def gnn(nc, x_in, src, dst, ea10, ea3, ew, W1, b1, W2, b2, Wl, bl, W3T, b3, R1, R2, cst, out, stop=4):
    from contextlib import ExitStack
    ctx = ExitStack()
    with ctx:
        def sb(name, shape, dt=F32):
            return ctx.enter_context(nc.sbuf_tensor(name, shape, dt))

        def ps(name, shape):
            return ctx.enter_context(nc.psum_tensor(name, shape, F32))

        def sem(name):
            return ctx.enter_context(nc.semaphore(name))

        def dram(name, shape, dt=F32):
            return nc.dram_tensor(name, shape, dt, kind="Internal").ap()

        tables = [x_in, dram("tab1", [NP, D]), dram("tab2", [NP, H]), dram("tab3", [NP, D]), dram("tab4", [NP, D])]
        width = [D, D, H, D, D]
        sums = [dram(f"sums{k}", [EP, width[k]]) for k in range(5)]
        radial_d = dram("radial", [P, T * P], BF16)

        cs = sb("cs", [P, BIG])
        ident, tri, before, iota = (cs[:, k * P:(k + 1) * P] for k in range(4))
        rows_of = [cs[:, 4 * P + k:4 * P + k + 1] for k in range(3)]
        edge0 = cs[:, 4 * P + 3:4 * P + 4]
        iota_b = sb("iota_b", [P, P], BF16)
        zero_b = sb("zero_b", [P, P], BF16)
        ones = sb("ones", [P, P])
        mask = sb("mask", [P, T])
        wgt = sb("wgt", [P, T])
        unit = sb("unit", [P, T * 3])
        big = sb("big", [P, 14080])
        grows = sb("grows", [P, 2 * C * H])
        idx = sb("idx", [P, 4 * C], I32)
        xs = sb("xs", [P, NT * D])
        own = sb("own", [P, NT * H])
        agg = sb("agg", [P, NT * H])
        carry = sb("carry", [P, H])
        fix = sb("fix", [P, H])
        same = sb("same", [P, P])
        firstd = sb("firstd", [P, 1])
        lastd = sb("lastd", [P, 1])
        ends = sb("ends", [P, NT], I32)
        end1 = sb("end1", [P, 1], I32)
        stat = sb("stat", [P, 8 * NT])
        posm = sb("posm", [P, NT])
        dinv = sb("dinv", [P, NT])
        blk1 = sb("blk1", [64, 96])
        blk2 = sb("blk2", [96, 96])
        blkl = sb("blkl", [96, 64])
        blk3 = sb("blk3", [64, 64])
        bias = sb("bias", [P, 2 * H + 2 * D])
        bias1, bias2 = bias[:, 0:H], bias[:, H:2 * H]
        biasl, bias3 = bias[:, 2 * H:2 * H + D], bias[:, 2 * H + D:]
        rw1 = sb("rw1", [10, P])
        rw1s = sb("rw1s", [10, RAD])
        wsp = sb("wsp", [P, 896], BF16)

        dstf = big[:, 0:T]
        dsti = big[:, T:2 * T].bitcast(I32)
        tmpi = big[:, 2 * T:3 * T].bitcast(I32)
        b_lo = big[:, 2 * T + T:3 * T + T // 2].bitcast(BF16)
        b_hi = big[:, 3 * T + T // 2:4 * T].bitcast(BF16)
        o = 4 * T
        onelo = [big[:, o + h * C * P // 2:o + (h + 1) * C * P // 2].bitcast(BF16) for h in range(2)]
        o += C * P
        onehi = [big[:, o + h * C * NT // 2:o + (h + 1) * C * NT // 2].bitcast(BF16) for h in range(2)]
        nrm = agg[:, 0:T]
        nrm2 = agg[:, T:2 * T]
        sq3 = big[:, 4 * T + 2688:4 * T + 2688 + T * 3]
        w8 = big[:, 4 * T:4 * T + 896]
        wc = big[:, 4 * T + 896:4 * T + 1792]
        wb1 = big[:, 4 * T + 1792:4 * T + 2240].bitcast(BF16)
        wb2 = big[:, 4 * T + 2240:4 * T + 2688].bitcast(BF16)
        QC = C // 4
        emb = [big[0:10, h * QC * QE:(h + 1) * QC * QE] for h in range(2)]
        hres = [big[:, 2 * QC * QE + k * QE:2 * QC * QE + (k + 1) * QE] for k in range(2)]
        o = 2 * QC * QE + 2 * QE
        hspl = [big[:, o + h * QC * QE // 2:o + (h + 1) * QC * QE // 2].bitcast(BF16) for h in range(2)]
        o += QC * QE
        hmid = big[:, o:o + QE // 2].bitcast(BF16)
        stage_in = big[:, 0:NB * H]
        stage_T = big[:, 1024:1024 + 7 * P]
        work = big[:, 2048:2048 + NT * D]
        own48 = big[:, 5248:5248 + NT * H]
        rad = [big[:, h * C3 * P // 2:(h + 1) * C3 * P // 2].bitcast(BF16) for h in range(2)]
        o = C3 * P
        prod = [big[:, o + k * 2 * MUL * 72:o + (k + 1) * 2 * MUL * 72] for k in range(2)]
        o += 4 * MUL * 72
        xsc = [big[:, o + h * C3 * 64:o + h * C3 * 64 + C3 * 16] for h in range(2)]
        xve = [big[:, o + h * C3 * 64 + C3 * 16:o + (h + 1) * C3 * 64] for h in range(2)]
        o += 2 * C3 * 64
        pm = big[:, o:o + C3 * 48]
        o += C3 * 48
        pr = [big[:, o + h * C3 * 16:o + (h + 1) * C3 * 16] for h in range(2)]
        o += 2 * C3 * 16
        red = [agg[:, k * B3 * 72:(k + 1) * B3 * 72] for k in range(2)]
        sc = [own[:, k * B3 * 24:(k + 1) * B3 * 24] for k in range(2)]
        th = [own[:, (48 + k * 16) * B3:(64 + k * 16) * B3] for k in range(2)]
        vec = [own[:, (80 + k * 24) * B3:(104 + k * 24) * B3] for k in range(2)]
        msg = big[:, o:o + T3 * D]
        o += T3 * D
        assert o <= 14080, o

        bank = [ps(f"bank{k}", [P, 512]) for k in range(8)]
        hist = bank[0][:, 0:NT]

        s_cst, s_small, s_dst, s_ea, s_w8, s_x, s_bias = (sem(n) for n in (
            "s_cst", "s_small", "s_dst", "s_ea", "s_w8", "s_x", "s_bias"))
        s_v = sem("vector_chain")
        s_blk0, s_blk = sem("blocks_zeroed"), sem("blocks_loaded")
        s_sq, s_root = sem("square_ready"), sem("root_ready")
        s_setup = sem("setup_done")
        s_idx = [[sem(f"idx_in{k}{h}") for h in range(2)] for k in range(5)]
        s_g = [[sem(f"rows_in{k}{h}") for h in range(2)] for k in range(5)]
        s_scan = [sem(f"scanned{k}") for k in range(5)]
        s_st = [[sem(f"sums_out{k}{h}") for h in range(2)] for k in range(5)]
        s_tab = sem("table_out")
        s_fixmm, s_fixin, s_fixsum, s_fixout, s_node = (sem(n) for n in (
            "carry_summed", "fix_rows_in", "fix_added", "fix_rows_out", "node_rows_in"))
        s_ends = sem("ends_ready")
        s_one, s_hist, s_h0 = sem("onehot_ready"), sem("hist_done"), sem("hist_first")
        s_cum, s_cumd = sem("counts_ready"), sem("prefix_done")
        s_same, s_samed = sem("diag_ready"), sem("diag_done")
        s_stage, s_tp, s_tc, s_mm = sem("stage_in"), sem("transposed"), sem("transposed_copied"), sem("stage_mm")
        s_emb = [sem("emb_in0"), sem("emb_in1")]
        s_hmm, s_hact, s_hdone, s_hout = sem("h_mm"), sem("h_act"), sem("h_split"), [sem("h_out0"), sem("h_out1")]
        s_tabrdy = sem("table_ready")
        s_out = sem("out")
        s_rad = [sem("rad_in0"), sem("rad_in1")]
        s_wmm, s_mul, s_red, s_redc, s_sc, s_th = sem("w_mm"), sem("products"), sem("reduced"), sem("reduced_copied"), sem("scalars"), sem("tanh_ready")
        s_xc = sem("x_compact")
        s_gate = {e: sem(f"gate_{e}") for e in ("pool", "sp", "act", "pe", "dve")}

        def gate(eng, who, s, v):
            eng.wait_ge(s, v)
            eng.sem_inc(s_gate[who], 1)

        stores = 0
        block = ctx.enter_context(nc.Block())

        def rows(ap, k):
            return ap.rearrange("p (t f) -> p t f", f=k)

        sums_v = [s.rearrange("(p t) f -> p (t f)", p=P) for s in sums]
        npass = min(5, stop + 1) if stop > 1 else stop
        passes = list(range({1: 1, 2: 3, 3: 4, 4: 5}[stop]))

        @block.sync
        def _(sp):
            sp.dma_start(cs[:, :], cst).then_inc(s_cst, 16)
            sp.dma_start(dsti, dst).then_inc(s_dst, 16)
            sp.dma_start(wgt[:, :], ew).then_inc(s_ea, 16)
            sp.dma_start(unit[:, :], ea3).then_inc(s_ea, 16)
            for g in range(8):
                sp.dma_start(w8[g * RAD:(g + 1) * RAD, :], R2).then_inc(s_w8, 16)
            sp.dma_start(rw1s[:, :], R1).then_inc(s_small, 16)
            sp.dma_start(rows(xs[:, :], D), x_in.rearrange("(j p) f -> p j f", p=P)).then_inc(s_x, 16)
            for b, s in ((b1, bias1), (b2, bias2), (bl, biasl), (b3, bias3)):
                sp.dma_start(s, b.to_broadcast([P, b.shape[1]])).then_inc(s_bias, 16)
            sp.wait_ge(s_blk0, 1)
            for m, W, fi, fo in ((blk1, W1, D, H), (blk2, W2, H, H), (blkl, Wl, H, D), (blk3, W3T, D, D)):
                for q in range(2):
                    sp.dma_start(m[q * fi:(q + 1) * fi, q * fo:(q + 1) * fo], W).then_inc(s_blk, 16)

            def pass_traffic(k, f):
                src_v = src
                half = C * f
                for h in range(2):
                    sp.dma_start(idx[:, h * C:(h + 1) * C], src_v[:, h * C:(h + 1) * C]).then_inc(s_idx[k][h], 16)

                def turn(i, last):
                    for h in range(2):
                        gate(sp, "sp", s_scan[k], 2 * i + h + 1)
                        sp.dma_start(sums_v[k][:, bass.ds((2 * i + h) * half, half)],
                                     grows[:, h * half:(h + 1) * half]).then_inc(s_st[k][h], 16)
                        if not last:
                            sp.dma_start(idx[:, h * C:(h + 1) * C],
                                         src_v[:, bass.ds((2 * i + 2 + h) * C, C)]).then_inc(s_idx[k][h], 16)
                        if k == 1:
                            gate(sp, "sp", s_hdone, QC * (2 * i + h + 1))
                            sp.dma_start(radial_d[:, bass.ds((2 * i + h) * (C * P), C * P)], hspl[h]).then_inc(s_hout[h], 16)
                            if not last:
                                sp.dma_start(emb[h], ea10[:, bass.ds((2 * i + 2 + h) * (C * P), C * P)]).then_inc(s_emb[h], 16)

                if k == 1:
                    for h in range(2):
                        sp.dma_start(emb[h], ea10[:, h * C * P:(h + 1) * C * P]).then_inc(s_emb[h], 16)
                with sp.Fori(0, NIT - 1) as i:
                    turn(i, False)
                turn(NIT - 1, True)

            def table_out(k, n):
                sp.wait_ge(s_tabrdy, n)
                f = width[k]
                a = xs if k == 4 else own
                sp.dma_start(tables[k].rearrange("(j p) f -> p j f", p=P), rows(a[:, 0:NT * f], f)).then_inc(s_tab, 16)

            n = 0
            for k in passes:
                if k == 4:
                    def load_idx(i, h):
                        for q, ind in enumerate((src, dst)):
                            sp.dma_start(idx[:, (2 * h + q) * C3:(2 * h + q + 1) * C3],
                                         ind[:, bass.ds(i * T3 + h * C3, C3)]).then_inc(s_idx[4][h], 16)

                    def load_rad(i, h):
                        sp.dma_start(rad[h], radial_d[:, bass.ds(i * (T3 * P) + h * C3 * P, C3 * P)]).then_inc(s_rad[h], 16)

                    def store(i):
                        gate(sp, "sp", s_scan[4], i + 1)
                        sp.dma_start(sums_v[4][:, bass.ds(i * (T3 * D), T3 * D)], msg).then_inc(s_st[4][0], 16)

                    def turn(i, prev, more, more2):
                        if prev:
                            store(i - 1)
                        if more:
                            gate(sp, "sp", s_xc, 2 * i + 2 + TOKENS)
                            load_idx(i + 1, 1)
                            gate(sp, "sp", s_mul, i * T3 + C3)
                            load_rad(i + 1, 0)
                        if more2:
                            gate(sp, "sp", s_xc, 2 * i + 3 + TOKENS)
                            load_idx(i + 2, 0)
                        if more:
                            gate(sp, "sp", s_mul, i * T3 + T3)
                            load_rad(i + 1, 1)

                    for h in range(2):
                        load_idx(0, h)
                        load_rad(0, h)
                    gate(sp, "sp", s_xc, 1 + TOKENS)
                    load_idx(1, 0)
                    turn(0, False, True, True)
                    with sp.Fori(1, NIT3 - 2) as i:
                        turn(i, True, True, True)
                    turn(NIT3 - 2, True, True, False)
                    turn(NIT3 - 1, True, False, False)
                    store(NIT3 - 1)
                else:
                    pass_traffic(k, width[k])
                if k + 1 in passes:
                    table_out(k + 1, k + 1)
            sp.wait_ge(s_tabrdy, len(passes))
            sp.dma_start(out.rearrange("(j p) f -> p j f", p=P), rows(xs[:, :], D)).then_inc(s_out, 16)
            sp.wait_ge(s_out, 16)

        @block.gpsimd
        def _(pool):
            for k in passes:
                f = width[k]
                if k:
                    pool.wait_ge(s_tab, 16 * k)
                if k < 4:
                    def turn(i, first):
                        for h in range(2):
                            gate(pool, "pool", s_idx[k][h], 16 * i + 16)
                            if not first:
                                gate(pool, "pool", s_st[k][h], 16 * i)
                            for j in range(C):
                                pool.indirect_dma_start(
                                    grows[:, (h * C + j) * f:(h * C + j + 1) * f], None, tables[k],
                                    bass.IndirectOffsetOnAxis(idx[:, h * C + j:h * C + j + 1], 0)).then_inc(s_g[k][h], 16)
                    turn(0, True)
                    with pool.Fori(1, NIT) as i:
                        turn(i, False)
                    turns = NIT
                else:
                    with pool.Fori(0, NIT3) as i:
                        for h in range(2):
                            gate(pool, "pool", s_idx[4][h], 32 * i + 32)
                            gate(pool, "pool", s_xc, 2 * i + h - 1 + TOKENS)
                            for j in range(C3):
                                for q in range(2):
                                    at = ((h * C3 + j) * 2 + q)
                                    pool.indirect_dma_start(
                                        grows[:, at * D:(at + 1) * D], None, tables[4],
                                        bass.IndirectOffsetOnAxis(idx[:, (2 * h + q) * C3 + j:(2 * h + q) * C3 + j + 1], 0)
                                    ).then_inc(s_g[4][h], 16)
                    turns = NIT3
                for h in range(1 if k == 4 else 2):
                    pool.wait_ge(s_st[k][h], 16 * turns)
                if k == 0:
                    pool.wait_ge(s_ends, 1)
                pool.indirect_dma_start(fix[:, 0:f], None, sums[k], bass.IndirectOffsetOnAxis(end1[:, 0:1], 0)).then_inc(s_fixin, 16)
                pool.wait_ge(s_fixsum, k + 1)
                pool.indirect_dma_start(sums[k], bass.IndirectOffsetOnAxis(end1[:, 0:1], 0), fix[:, 0:f], None).then_inc(s_fixout, 16)
                pool.wait_ge(s_fixout, 16 * (k + 1))
                if k == 0:
                    pool.wait_ge(s_ends, 2)
                for j in range(NT):
                    pool.indirect_dma_start(agg[:, j * f:(j + 1) * f], None, sums[k],
                                            bass.IndirectOffsetOnAxis(ends[:, j:j + 1], 0)).then_inc(s_node, 16)

        @block.scalar
        def _(act):
            act.wait_ge(s_sq, 1)
            act.activation(nrm, nrm, ACT.Sqrt).then_inc(s_root, 1)
            roots = 1

            for k in passes:
                if k == 0:
                    act.wait_ge(s_sq, roots + 1)
                    act.activation(stat[:, NT:2 * NT], stat[:, 0:NT], ACT.Sqrt).then_inc(s_root, 1)
                    roots += 1
                if k == 1:
                    def turn(i, first):
                        for h in range(2):
                            if not first:
                                gate(act, "act", s_hout[h], 16 * i)
                            for q in range(QC):
                                n = (2 * i + h) * QC + q
                                gate(act, "act", s_hmm, n + 1)
                                pb = bank[2 + (h * QC + q) % 2][:, :]
                                act.activation(hspl[h][:, q * QE:(q + 1) * QE], pb, ACT.Relu, scale=RADIAL_SCALE).then_inc(s_hact, 1)
                                if not (first and h == 0 and q < 2):
                                    gate(act, "act", s_hdone, n - 1)
                                act.activation(hres[(h * QC + q) % 2], pb, ACT.Relu, scale=RADIAL_SCALE).then_inc(s_hact, 1)
                    turn(0, True)
                    with act.Fori(1, NIT) as i:
                        turn(i, False)
                if k == 4:
                    act.sem_inc(s_xc, TOKENS)
                    act.sem_inc(s_redc, TOKENS)

                    def compact(i, h, wait):
                        gate(act, "act", s_g[4][h], 16 * 2 * C3 * (i + 1))
                        if wait:
                            gate(act, "act", s_mul, i * T3 + h * C3 - C3)
                        g = rows(grows[:, h * C3 * 64:(h + 1) * C3 * 64], D)
                        act.copy(rows(xsc[h], 8), g[:, :, 0:8])
                        act.copy(rows(xve[h], 24), g[:, :, 8:32]).then_inc(s_xc, 1)

                    def batch(i, b):
                        n = 4 * i + b
                        gate(act, "act", s_red, B3 // 2 * n + B3 // 2)
                        if not (isinstance(i, int) and n < 2):
                            gate(act, "act", s_sc, 2 * n - 2)
                        act.copy(red[b % 2], bank[4 + b % 2][:, 0:B3 * 72]).then_inc(s_redc, 1)
                        gate(act, "act", s_sc, 2 * n + 1)
                        act.activation(rows(th[b % 2], 16), rows(sc[b % 2], 24)[:, :, 0:16], ACT.Tanh).then_inc(s_th, 1)

                    def turn(i, first, last):
                        if not first:
                            batch(i - 1, 3)
                        compact(i, 1, not first)
                        batch(i, 0)
                        batch(i, 1)
                        if not last:
                            compact(i + 1, 0, True)
                        batch(i, 2)

                    compact(0, 0, False)
                    turn(0, True, False)
                    with act.Fori(1, NIT3 - 1) as i:
                        turn(i, False, False)
                    turn(NIT3 - 1, False, True)
                    batch(NIT3 - 1, 3)
                for st in {0: [], 1: [0], 2: [1, 2], 3: [3], 4: []}[k]:
                    fi = (D, H, H, D)[st]
                    with act.Fori(0, NBLK) as b:
                        gate(act, "act", s_tp, st * NBLK + b + 1)
                        act.copy(stage_T[0:2 * fi, 0:4 * P], bank[0][0:2 * fi, :])
                        act.copy(stage_T[0:2 * fi, 4 * P:7 * P], bank[1][0:2 * fi, 0:3 * P]).then_inc(s_tc, 1)
                if k != 1:
                    act.wait_ge(s_sq, roots + 1)
                    act.activation(stat[:, NT:2 * NT], stat[:, 0:NT], ACT.Sqrt).then_inc(s_root, 1)
                    roots += 1

        @block.vector
        def _(v):
            ch = Chain(v, s_v)
            TT, TS = v.tensor_tensor, v.tensor_scalar

            def step(ins):
                ch.inc(ins)
                ch.sync()

            for m in (blk1, blk2, blkl, blk3):
                last = v.memset(m[:, :], 0.0)
            ch.inc(last)
            ch.sync()
            v.sem_inc(s_blk0, 1)
            v.wait_ge(s_cst, 16)
            v.wait_ge(s_dst, 16)
            step(v.tensor_copy(dstf, dsti))
            v.tensor_copy(iota_b[:, :], iota)
            v.memset(mask[:, 0:1], 0.0)
            v.tensor_copy(firstd[:, :], dstf[:, 0:1])
            v.tensor_copy(lastd[:, :], dstf[:, T - 1:T])
            TT(mask[:, 1:T], dstf[:, 1:T], dstf[:, 0:T - 1], ALU.is_equal)
            step(v.tensor_single_scalar(tmpi, dsti, 7, ALU.logical_shift_right))
            step(v.tensor_copy(b_hi, tmpi))
            step(v.tensor_single_scalar(tmpi, dsti, 127, ALU.bitwise_and))
            step(v.tensor_copy(b_lo, tmpi))
            step(TS(agg[:, 0:T], dstf, firstd[:, 0:1], None, ALU.is_equal))
            step(v.tensor_reduce(stat[:, 0:1], agg[:, 0:T], axis=AX.X, op=ALU.add))
            step(TS(stat[:, 1:2], stat[:, 0:1], edge0, -1.0, ALU.add, ALU.add))
            v.tensor_copy(end1[:, :], stat[:, 1:2])
            step(TS(same[:, :], ident, firstd[:, 0:1], None, ALU.mult))
            v.memset(ones[:, :], 1.0).then_inc(s_same, 1)
            v.wait_ge(s_samed, 1)
            step(TS(same[:, :], bank[1][:, 0:P], lastd[:, 0:1], None, ALU.is_equal))
            TT(same[:, :], same[:, :], before, ALU.mult).then_inc(s_ends, 1)
            v.wait_ge(s_ea, 32)
            step(TT(sq3, unit[:, :], unit[:, :], ALU.mult))
            v.tensor_reduce(nrm2, rows(sq3, 3), axis=AX.X, op=ALU.add)
            v.tensor_reduce(nrm, rows(sq3, 3), axis=AX.X, op=ALU.add).then_inc(s_sq, 1)

            def refine(y, d, t):
                step(v.reciprocal(y, y))
                step(TT(t, y, y, ALU.mult))
                step(TT(t, t, d, ALU.mult))
                step(TS(t, t, -0.5, 1.5, ALU.mult, ALU.add))
                step(TT(y, y, t, ALU.mult))

            v.wait_ge(s_w8, 128)
            wv = w8.rearrange("p (k u w) -> p k u w", k=7, u=MUL)
            ab = wc[:, 0:WA].rearrange("p (u c) -> p u c", c=24)
            pb_ = wc[:, WA:WA + WB].rearrange("p (u c) -> p u c", c=24)
            fv = wc[:, WA + WB:896].rearrange("p (u c) -> p u c", c=8)
            for blk, dest, at, scale in ((0, ab, 0, PW_S), (2, ab, 8, PW_S), (4, ab, 16, PW_V),
                                         (1, pb_, 0, PW_S), (3, pb_, 8, PW_S), (6, pb_, 16, PW_V * 1.5 ** 0.5)):
                TS(dest[:, :, at:at + 8], wv[:, blk, :, :], scale, None, ALU.mult)
            step(TS(fv, wv[:, 6, :, :], -PW_V * 1.5 ** 0.5 / 3.0, None, ALU.mult))
            step(v.scalar_tensor_tensor(out=fv, in0=wv[:, 5, :, :], scalar=PW_V * INV_SQRT3, in1=fv, op0=ALU.mult, op1=ALU.add))
            step(v.tensor_copy(wb1, wc))
            step(TT(wc, wc, wb1, ALU.subtract))
            step(v.tensor_copy(wb2, wc))
            step(TT(wc, wc, wb2, ALU.subtract))
            step(TS(wsp[:, :], wc, rows_of[2], None, ALU.mult))
            step(v.scalar_tensor_tensor(out=wsp[:, :], in0=wb2, scalar=rows_of[1], in1=wsp[:, :], op0=ALU.mult, op1=ALU.add))
            step(v.scalar_tensor_tensor(out=wsp[:, :], in0=wb1, scalar=rows_of[0], in1=wsp[:, :], op0=ALU.mult, op1=ALU.add))
            v.wait_ge(s_small, 16)
            step(v.tensor_copy(rw1[:, :].rearrange("k (g r) -> k g r", g=8), bc(rw1s[:, :], 1, 8)))
            v.wait_ge(s_root, 1)
            refine(nrm, nrm2, own[:, 0:T])
            step(TT(rows(unit[:, :], 3), rows(unit[:, :], 3), bc(nrm, 2, 3), ALU.mult))
            v.memset(zero_b[:, :], 0.0).then_inc(s_h0, 1)
            roots = 1

            def scans(k, f, rowsbuf, i, h, cols):
                m = mask[:, bass.ds((2 * i + h) * cols, cols)]
                for c in range(f):
                    last = v.tensor_tensor_scan(out=rowsbuf[:, :, c], data0=m, data1=rowsbuf[:, :, c],
                                                initial=carry[:, c:c + 1], op0=ALU.mult, op1=ALU.add)
                step(last)
                step(v.tensor_copy(carry[:, 0:f], rowsbuf[:, cols - 1, :]))
                v.sem_inc(s_scan[k], 1)

            def newton_norm(x):
                nonlocal roots
                x3, w3 = rows(x, D), rows(work, D)
                s0, s1, s2, s3 = (stat[:, q * NT:(q + 1) * NT] for q in range(4))
                step(v.tensor_reduce(s2, x3, axis=AX.X, op=ALU.add))
                step(TS(s2, s2, 1.0 / D, None, ALU.mult))
                step(TT(x3, x3, bc(s2, 2, D), ALU.subtract))
                step(TT(work, x, x, ALU.mult))
                step(v.tensor_reduce(s2, w3, axis=AX.X, op=ALU.add))
                TS(s0, s2, 1.0 / D, EPS, ALU.mult, ALU.add).then_inc(s_sq, 1)
                roots += 1
                v.wait_ge(s_root, roots)
                refine(s1, s0, s3)
                step(TT(x3, x3, bc(s1, 2, D), ALU.mult))

            for k in passes:
                f = width[k]
                step(v.memset(carry[:, :], 0.0))
                if k < 4:
                    half = C * f

                    def body(i, h):
                        g = rows(grows[:, h * half:(h + 1) * half], f)
                        v.wait_ge(s_g[k][h], 16 * C * (i + 1))
                        if k == 0:
                            step(TT(g, g, bc(wgt[:, bass.ds((2 * i + h) * C, C)], 2, f), ALU.mult))
                        else:
                            v.sem_inc(s_gate["dve"], 1)
                        scans(k, f, g, i, h, C)
                        if k == 0:
                            gate(v, "dve", s_hist, 2 * i + 1)
                            lo = b_lo[:, bass.ds((2 * i + h) * C, C)]
                            hi = b_hi[:, bass.ds((2 * i + h) * C, C)]
                            TT(onelo[h].rearrange("p (t c) -> p t c", c=P), bc(lo, 2, P), bc(iota_b[:, :], 1, C), ALU.is_equal)
                            TT(onehi[h].rearrange("p (t c) -> p t c", c=NT), bc(hi, 2, NT), bc(iota_b[:, 0:NT], 1, C), ALU.is_equal).then_inc(s_one, 1)
                        if k == 1:
                            for q in range(QC):
                                n = (2 * i + h) * QC + q
                                hs = hspl[h][:, q * QE:(q + 1) * QE]
                                hr = hres[(h * QC + q) % 2]
                                v.wait_ge(s_hact, 2 * n + 2)
                                step(TT(hr, hr, hs, ALU.subtract))
                                step(v.tensor_copy(hmid, hr))
                                v.tensor_copy(hs[32:64, :], hmid[32:64, :])
                                TT(hs[96:128, :], hr[96:128, :], hmid[96:128, :], ALU.subtract).then_inc(s_hdone, 1)

                    per = {0: 6, 1: 2 * (2 + 2 * QC), 2: 4, 3: 4}[k]
                    with v.Fori(0, NIT) as i:
                        ch.enter(i, per)
                        for h in range(2):
                            body(i, h)
                    ch.leave(NIT)
                else:
                    def project(i, h):
                        v.wait_ge(s_xc, 2 * i + h + 1 + TOKENS)
                        v.sem_inc(s_gate["dve"], 1)
                        xv4 = xve[h].rearrange("p (t u i) -> p t u i", u=MUL, i=3)
                        pm4 = pm.rearrange("p (t u i) -> p t u i", u=MUL, i=3)
                        nv = rows(unit[:, bass.ds(i * (T3 * 3) + h * C3 * 3, C3 * 3)], 3)
                        step(TT(pm4, xv4, bc(nv, 2, MUL), ALU.mult))
                        step(v.tensor_reduce(rows(pr[h], MUL), pm4, axis=AX.X, op=ALU.add))

                    def products(i, t):
                        h, th_ = t // C3, t % C3
                        q = t % 2
                        pk = prod[t // 2 % 2][:, t % 2 * MUL * 72:(t % 2 + 1) * MUL * 72].rearrange("p (u c) -> p u c", c=72)
                        v.wait_ge(s_wmm, i * T3 + t + 1)
                        TT(pk[:, :, 0:24], bank[q][:, 0:WA].rearrange("p (u c) -> p u c", c=24),
                           bc(xsc[h][:, th_ * MUL:(th_ + 1) * MUL], 2, 24), ALU.mult)
                        TT(pk[:, :, 24:48], bank[2 + q][:, 0:WB].rearrange("p (u c) -> p u c", c=24),
                           bc(pr[h][:, th_ * MUL:(th_ + 1) * MUL], 2, 24), ALU.mult)
                        TT(pk[:, :, 48:72].rearrange("p u (i w) -> p u i w", i=3),
                           bc(bank[2 + q][:, WB:512].rearrange("p (u w) -> p u w", w=8), 2, 3),
                           bc(xve[h][:, th_ * 48:(th_ + 1) * 48].rearrange("p (u i) -> p u i", i=3), 3, 8),
                           ALU.mult).then_inc(s_mul, 1)

                    def scalars(i, b):
                        r = rows(red[b % 2], 72)
                        v.wait_ge(s_redc, 4 * i + b + 1 + TOKENS)
                        TT(rows(sc[b % 2], 24), r[:, :, 0:24], r[:, :, 24:48], ALU.add).then_inc(s_sc, 1)

                    def messages(i, b, wait):
                        n = 4 * i + b
                        r, s_, t_, e_ = (rows(a[b % 2], w) for a, w in ((red, 72), (sc, 24), (th, 16), (vec, 24)))
                        cols = bass.ds(i * T3 + b * B3, B3)
                        mg = rows(msg, D)[:, b * B3:(b + 1) * B3, :]
                        mv = mg[:, :, 8:32].rearrange("p t (w i) -> p t i w", i=3)
                        if wait:
                            gate(v, "dve", s_st[4][0], 16 * i)
                        v.wait_ge(s_th, n + 1)
                        v.scalar_tensor_tensor(out=mg[:, :, 0:8], in0=t_[:, :, 0:8], scalar=TANH_GAIN, in1=bc(wgt[:, cols], 2, 8),
                                               op0=ALU.mult, op1=ALU.mult)
                        ch.inc(v.scalar_tensor_tensor(out=t_[:, :, 8:16], in0=t_[:, :, 8:16], scalar=TANH_GAIN,
                                                      in1=bc(wgt[:, cols], 2, 8), op0=ALU.mult, op1=ALU.mult))
                        e4 = e_.rearrange("p t (i w) -> p t i w", i=3)
                        nb = rows(unit[:, bass.ds(i * (T3 * 3) + b * B3 * 3, B3 * 3)], 3)
                        step(TT(e4, bc(s_[:, :, 16:24], 2, 3), bc(nb, 3, 8), ALU.mult))
                        step(TT(e_, e_, r[:, :, 48:72], ALU.add))
                        TT(mv, e4, bc(t_[:, :, 8:16], 2, 3), ALU.mult).then_inc(s_sc, 1)

                    def scan_part(i, part):
                        m = mask[:, bass.ds(i * T3, T3)]
                        mr = rows(msg, D)
                        if part == 0:
                            v.wait_ge(s_sc, 8 * i + 8)
                            v.sem_inc(s_gate["dve"], 1)
                        for c in range(part * 8, part * 8 + 8):
                            last = v.tensor_tensor_scan(out=mr[:, :, c], data0=m, data1=mr[:, :, c],
                                                        initial=carry[:, c:c + 1], op0=ALU.mult, op1=ALU.add)
                        if part == 3:
                            step(last)
                            step(v.tensor_copy(carry[:, 0:D], mr[:, T3 - 1, :]))
                            v.sem_inc(s_scan[4], 1)

                    def turn(i, first, last):
                        for t in range(T3):
                            products(i, t)
                            if not first and t == LAG:
                                scalars(i - 1, 3)
                            if not first and t == LAG + 1:
                                messages(i - 1, 3, False)
                            if not first and LAG + 1 <= t < LAG + 5:
                                scan_part(i - 1, t - LAG - 1)
                            for b in range(3):
                                if t == (b + 1) * B3 + LAG:
                                    scalars(i, b)
                                if t == (b + 1) * B3 + LAG + 1:
                                    messages(i, b, b == 0 and not first)
                            if t == C3 - 2:
                                project(i, 1)
                            if t == T3 - 1 and not last:
                                project(i + 1, 0)

                    project(0, 0)
                    turn(0, True, False)
                    per, start = 4 * 3 + 2 + 4, ch.k
                    with v.Fori(1, NIT3 - 1) as i:
                        ch.per, ch.start = per, start
                        ch.base, ch.k = (i - 1) * per + start, 0
                        turn(i, False, False)
                    ch.leave(NIT3 - 2)
                    turn(NIT3 - 1, False, True)
                    scalars(NIT3 - 1, 3)
                    messages(NIT3 - 1, 3, False)
                    for part in range(4):
                        scan_part(NIT3 - 1, part)

                if k == 0:
                    v.wait_ge(s_hist, 2 * NIT + 2)
                    cnt = stat[:, 2 * NT:3 * NT]
                    step(v.tensor_copy(cnt, hist))
                    v.sem_inc(s_cum, 1)
                    step(TS(posm[:, :], cnt, 1.0, None, ALU.min))
                    TS(stat[:, 0:NT], cnt, 1.0, None, ALU.add).then_inc(s_sq, 1)
                    v.wait_ge(s_cumd, 1)
                    step(v.tensor_copy(stat[:, 3 * NT:4 * NT], bank[1][:, NT:2 * NT]))
                    step(v.memset(stat[:, 5 * NT:6 * NT], 1.0))
                    step(v.tensor_tensor_scan(out=stat[:, 4 * NT:5 * NT], data0=stat[:, 5 * NT:6 * NT], data1=stat[:, 3 * NT:4 * NT],
                                              initial=0.0, op0=ALU.mult, op1=ALU.add))
                    step(TT(stat[:, 4 * NT:5 * NT], stat[:, 4 * NT:5 * NT], stat[:, 3 * NT:4 * NT], ALU.subtract))
                    step(TT(stat[:, 4 * NT:5 * NT], stat[:, 4 * NT:5 * NT], bank[1][:, 0:NT], ALU.add))
                    step(TS(stat[:, 4 * NT:5 * NT], stat[:, 4 * NT:5 * NT], -1.0, 0.0, ALU.add, ALU.max))
                    v.tensor_copy(ends[:, :], stat[:, 4 * NT:5 * NT]).then_inc(s_ends, 1)
                    roots += 1
                    v.wait_ge(s_root, roots)
                    step(v.tensor_copy(dinv[:, :], stat[:, NT:2 * NT]))
                    refine(dinv[:, :], stat[:, 0:NT], stat[:, 5 * NT:6 * NT])
                v.wait_ge(s_fixin, 16 * (k + 1))
                v.wait_ge(s_fixmm, k + 1)
                TT(fix[:, 0:f], fix[:, 0:f], bank[7][:, 0:f], ALU.add).then_inc(s_fixsum, 1)
                v.wait_ge(s_node, 16 * NT * (k + 1))
                if k == 0:
                    v.wait_ge(s_x, 16)
                    v.wait_ge(s_bias, 64)
                if k == 1:
                    for h in range(2):
                        v.wait_ge(s_hout[h], 16 * NIT)
                a3 = rows(agg[:, 0:NT * f], f)
                o3 = rows(own[:, 0:NT * f], f)
                step(TT(a3, a3, bc(posm[:, :], 2, f), ALU.mult))
                if k == 0:
                    step(v.scalar_tensor_tensor(out=xs[:, :], in0=xs[:, :], scalar=2.0, in1=agg[:, 0:NT * D], op0=ALU.mult, op1=ALU.add))
                    newton_norm(xs[:, :])
                    step(TT(o3, rows(xs[:, :], D), bc(dinv[:, :], 2, D), ALU.mult))
                elif k < 4:
                    for st in {1: [0], 2: [1, 2], 3: [3]}[k]:
                        fi, fo = ((D, H), (H, H), (H, D), (D, D))[st]
                        per = {0: 6, 1: 5, 2: 3, 3: 6}[st]
                        with v.Fori(0, NBLK) as b:
                            ch.enter(b, per)
                            n = st * NBLK + b
                            si = rows(stage_in[:, 0:NB * fi], fi)
                            a = rows(agg[:, bass.ds(b * (NB * fi), NB * fi)], fi)
                            o_ = rows(own[:, bass.ds(b * (NB * fi), NB * fi)], fi)
                            dv = dinv[:, bass.ds(b * NB, NB)]
                            if st == 2:
                                ch.inc(v.tensor_copy(si, a))
                            else:
                                step(TT(si, a, o_, ALU.add))
                                ch.inc(TT(si, si, bc(dv, 2, fi), ALU.mult))
                            ch.sync()
                            v.sem_inc(s_stage, 1)
                            v.wait_ge(s_mm, n + 1)
                            v.sem_inc(s_gate["dve"], 1)
                            for part, (bk, c0, cn) in enumerate(((2, 0, 8), (3, 8, 6))):
                                pv = rows(bank[bk][:, 0:cn * fo], fo)
                                if st == 0 or st == 1:
                                    bb = bias1 if st == 0 else bias2
                                    w_ = rows(work[:, c0 * fo:(c0 + cn) * fo], fo)
                                    last = TT(w_, pv, bc(bb, 1, cn), ALU.add)
                                else:
                                    bb = biasl if st == 2 else bias3
                                    w_ = rows(work[:, c0 * fo:(c0 + cn) * fo], fo)
                                    last = TT(w_, pv, bc(bb, 1, cn), ALU.add)
                            step(last)
                            wk = work[:, 0:NB * fo]
                            if st in (0, 1):
                                dst_t = own48 if st == 0 else agg
                                dd = dst_t[:, bass.ds(b * (NB * fo), NB * fo)]
                                if st == 0:
                                    step(v.scalar_tensor_tensor(out=wk, in0=wk, scalar=SLOPE, in1=wk, op0=ALU.mult, op1=ALU.max))
                                    step(TT(rows(dd, fo), rows(wk, fo), bc(dv, 2, fo), ALU.mult))
                                    step(v.memset(stat[:, 7 * NT:7 * NT + 1], 0.0))
                                else:
                                    step(v.scalar_tensor_tensor(out=dd, in0=wk, scalar=SLOPE, in1=wk, op0=ALU.mult, op1=ALU.max))
                                    step(v.memset(stat[:, 7 * NT:7 * NT + 1], 0.0))
                            else:
                                xx = xs[:, bass.ds(b * (NB * fo), NB * fo)]
                                if st == 3:
                                    step(TS(wk, wk, 0.0, None, ALU.max))
                                    step(v.memset(stat[:, 7 * NT:7 * NT + 1], 0.0))
                                step(TT(xx, xx, wk, ALU.add))
                        ch.leave(NBLK)
                    if k == 1:
                        step(v.tensor_copy(own[:, :], own48))
                    if k >= 2:
                        newton_norm(xs[:, :])
                    if k == 2:
                        step(TT(rows(own[:, 0:NT * D], D), rows(xs[:, :], D), bc(dinv[:, :], 2, D), ALU.mult))
                else:
                    step(TT(xs[:, :], xs[:, :], agg[:, 0:NT * D], ALU.add))
                    newton_norm(xs[:, :])
                v.sem_inc(s_tabrdy, 1)

        @block.tensor
        def _(pe):
            pe.wait_ge(s_same, 1)
            pe.wait_ge(s_cst, 16)
            pe.matmul(bank[1][:, 0:P], ones[:, :], same[:, :], start=True, stop=True).then_inc(s_samed, 1)
            for k in passes:
                f = width[k]
                if k == 0:
                    pe.wait_ge(s_h0, 1)
                    pe.matmul(hist, zero_b[:, :], zero_b[:, 0:NT], start=True, stop=False).then_inc(s_hist, 1)
                    with pe.Fori(0, NIT) as i:
                        for h in range(2):
                            gate(pe, "pe", s_one, 2 * i + h + 1)
                            for j in range(C):
                                last = pe.matmul(hist, onelo[h][:, j * P:(j + 1) * P], onehi[h][:, j * NT:(j + 1) * NT],
                                                 start=False, stop=False)
                            last.then_inc(s_hist, 1)
                    pe.matmul(hist, zero_b[:, :], zero_b[:, 0:NT], start=False, stop=True).then_inc(s_hist, 1)
                    pe.wait_ge(s_cum, 1)
                    cnt = stat[:, 2 * NT:3 * NT]
                    pe.matmul(bank[1][:, 0:NT], tri, cnt, start=True, stop=True)
                    pe.matmul(bank[1][:, NT:2 * NT], ones[:, :], cnt, start=True, stop=True).then_inc(s_cumd, 1)
                if k == 1:
                    def turn(i, first):
                        for h in range(2):
                            gate(pe, "pe", s_emb[h], 16 * i + 16)
                            for q in range(QC):
                                n = (2 * i + h) * QC + q
                                if not (first and h == 0 and q < 2):
                                    gate(pe, "pe", s_hact, 2 * (n - 1))
                                pe.matmul(bank[2 + (h * QC + q) % 2][:, :], rw1[:, :], emb[h][:, q * QE:(q + 1) * QE],
                                          start=True, stop=True).then_inc(s_hmm, 1)
                    turn(0, True)
                    with pe.Fori(1, NIT) as i:
                        turn(i, False)
                if k == 4:
                    def weights(i, t):
                        h = t // C3
                        if t % C3 == 0:
                            gate(pe, "pe", s_rad[h], 16 * i + 16)
                        lt = rad[h][:, (t % C3) * P:(t % C3 + 1) * P]
                        pe.matmul(bank[t % 2][:, 0:WA], lt, wsp[:, 0:WA], start=True, stop=True)
                        pe.matmul(bank[2 + t % 2][:, :], lt, wsp[:, WA:896], start=True, stop=True).then_inc(s_wmm, 1)

                    def reduce(i, t):
                        b, j = t // B3, t % B3
                        if j == 1:
                            gate(pe, "pe", s_redc, 4 * i + b - 1 + TOKENS)
                        pv = prod[t // 2 % 2].rearrange("p (t u c) -> p t u c", t=2, c=72)
                        for u in range(MUL):
                            last = pe.matmul(bank[4 + b % 2][:, (j - 1) * 72:(j + 1) * 72], ident, pv[:, :, u, :],
                                             start=(u == 0), stop=(u == MUL - 1))
                        last.then_inc(s_red, 1)

                    def turn(i, last):
                        for t in range(T3):
                            gate(pe, "pe", s_mul, i * T3 + t + 1)
                            if t + 2 < T3:
                                weights(i, t + 2)
                            elif not last:
                                weights(i + 1, t + 2 - T3)
                            if t % 2:
                                reduce(i, t)

                    weights(0, 0)
                    weights(0, 1)
                    with pe.Fori(0, NIT3 - 1) as i:
                        turn(i, False)
                    turn(NIT3 - 1, True)
                pe.wait_ge(s_scan[k], NIT3 if k == 4 else 2 * NIT)
                pe.matmul(bank[7][:, 0:f], same[:, :], carry[:, 0:f], start=True, stop=True).then_inc(s_fixmm, 1)
                for st in {0: [], 1: [0], 2: [1, 2], 3: [3], 4: []}[k]:
                    fi, fo = ((D, H), (H, H), (H, D), (D, D))[st]
                    wb = (blk1, blk2, blkl, blk3)[st]
                    if st == 0:
                        pe.wait_ge(s_blk, 128)
                    with pe.Fori(0, NBLK) as b:
                        gate(pe, "pe", s_stage, st * NBLK + b + 1)
                        for q in range(7):
                            last = pe.transpose(bank[q // 4][0:2 * fi, (q % 4) * P:(q % 4 + 1) * P],
                                                stage_in[:, q * 2 * fi:(q + 1) * 2 * fi], ident)
                        last.then_inc(s_tp, 1)
                        gate(pe, "pe", s_tc, st * NBLK + b + 1)
                        for q in range(7):
                            last = pe.matmul(bank[2 + q // 4][:, (q % 4) * 2 * fo:(q % 4 + 1) * 2 * fo],
                                             stage_T[0:2 * fi, q * P:(q + 1) * P], wb[:, :], start=True, stop=True)
                        last.then_inc(s_mm, 1)


def kernel(x, src, dst, edge_attr_10, edge_attr_3, edge_weight, L1_gnn_W1, L1_gnn_b1, L1_gnn_W2, L1_gnn_b2,
           L1_gnn_Wl, L1_gnn_bl, L2_gnn_W, L2_gnn_bias, L3_gnn_W1, L3_gnn_W2):
    import numpy as _np
    import concourse.bacc as _bacc
    from concourse.bass_utils import run_bass_kernel_spmd as _run

    def edges(a, fill):
        a = _np.asarray(a)
        a = _np.concatenate([a, _np.full((EP - E,) + a.shape[1:], fill, a.dtype)])
        return a.reshape((P, T) + a.shape[1:])

    cst = _np.zeros((P, BIG), _np.float32)
    cst[:, 0:P] = _np.eye(P)
    cst[:, P:2 * P] = _np.triu(_np.ones((P, P)))
    cst[:, 2 * P:3 * P] = _np.triu(_np.ones((P, P)), 1)
    cst[:, 3 * P:4 * P] = _np.arange(P)
    parts = [0] * 16 + [1] * 16 + [0] * 16 + [1] * 16 + [2] * 16 + [-1] * 16 + [0] * 16 + [-1] * 16
    for k in range(3):
        cst[:, 4 * P + k] = _np.array([q == k for q in parts])
    cst[:, 4 * P + 3] = _np.arange(P) * T
    x = _np.asarray(x)
    arrays = {
        "x": _np.concatenate([x, _np.zeros((NP - N, D), x.dtype)]),
        "src": edges(src, 0), "dst": edges(dst, N),
        "ea10": _np.ascontiguousarray(edges(edge_attr_10, 0).transpose(2, 1, 0).reshape(10, T * P)),
        "ea3": edges(edge_attr_3, 1).reshape(P, T * 3), "ew": edges(edge_weight, 0),
        "W1": L1_gnn_W1, "b1": _np.asarray(L1_gnn_b1).reshape(1, H), "W2": L1_gnn_W2, "b2": _np.asarray(L1_gnn_b2).reshape(1, H),
        "Wl": L1_gnn_Wl, "bl": _np.asarray(L1_gnn_bl).reshape(1, D), "W3T": _np.ascontiguousarray(_np.asarray(L2_gnn_W).T),
        "b3": _np.asarray(L2_gnn_bias).reshape(1, D), "R1": L3_gnn_W1, "R2": L3_gnn_W2, "cst": cst,
    }
    arrays = {f"in_{n}": _np.ascontiguousarray(a) for n, a in arrays.items()}
    nc = _bacc.Bacc("TRN2", target_bir_lowering=False, num_devices=1)
    args = [nc.dram_tensor(n, a.shape, mybir.dt.from_np(a.dtype), kind="ExternalInput").ap() for n, a in arrays.items()]
    args.append(nc.dram_tensor("out_x", (NP, D), F32, kind="ExternalOutput").ap())
    gnn(nc, *args, stop=STOP)
    r = _run(nc, [arrays], core_ids=[0])
    return r.results[0]["out_x"][0:N]
```

```python
import numpy as np
import concourse.bass as bass
from concourse import mybir

F32 = mybir.dt.float32
BF16 = mybir.dt.bfloat16
I32 = mybir.dt.int32
ALU = mybir.AluOpType
ACT = mybir.ActivationFunctionType
AX = mybir.AxisListType

P = 128
N, E, D, H = 12500, 200000, 32, 48
NT = -(-N // P)
NP = NT * P
T = 1584
EP = T * P
C = 24
NIT = T // C // 2
C3 = 24
T3 = 2 * C3
NIT3 = T // T3
B3 = 6
NB3 = T3 // B3
G3 = 3
GB = B3 // G3
MUL = 16
WA, WB, WF = MUL * 24, MUL * 24, MUL * 8
PC = 54
VC = PC - 48
RC = 72 - PC
AU = 4
SUM_AT = 3
SCAN_AT, FILL_AT = 6, 22
SC, FC = 2, 2
XC1_AT, XC0_AT = 11, 39
GATHERS = ((1, 0), (20, 0), (1, 0), (1, 1), (3, 3), (3, 3), (3, 3), (3, 3))
NB = 14
NBLK = NT // NB
QE = 4 * P
RAD = 16
SLOPE = (1.0 / 8.0 + 1.0 / 3.0) / 2.0
EPS = 1e-5
STAGES = {0: [], 1: [0], 2: [1, 2], 3: [3], 4: []}
STAGE_NO = {1: 0, 2: NBLK, 3: 3 * NBLK}
FI, FO = (D, H, H, D), (H, H, D, D)
NORMED = (0, 2, 3, 4)
TOKENS = 2
PASSES = 5
PW_S, PW_V, INV_SQRT3, TANH_GAIN = 0.17677669529663687, 0.25, 0.5773502691896258, 1.593
RADIAL_SCALE = 2.0 ** 0.5 / 10.0 ** 0.5 / 16.0 ** 0.5
BIG = 3 * P + P + 4 + NT


class Chain:

    def __init__(self, eng, sem):
        self.eng, self.sem, self.base, self.k = eng, sem, 0, 0

    def inc(self, ins):
        ins.then_inc(self.sem, 1)
        self.k += 1

    def sync(self):
        self.eng.wait_ge(self.sem, self.base + self.k)

    def enter(self, i, per):
        self.start, self.per = self.k, per
        self.base, self.k = i * per + self.start, 0

    def leave(self, turns):
        assert self.k == self.per, (self.k, self.per)
        self.base, self.k = 0, self.start + turns * self.per


def bc(ap, axis, n):
    v = ap.unsqueeze(axis)
    shape = list(v.shape)
    shape[axis] = n
    return v.to_broadcast(shape)


def gnn(nc, x_in, src, dst, ea10, ea3, ew, W1, b1, W2, b2, Wl, bl, W3T, b3, R1, R2, cst, out):
    from contextlib import ExitStack
    ctx = ExitStack()
    with ctx:
        def sb(name, shape, dt=F32):
            return ctx.enter_context(nc.sbuf_tensor(name, shape, dt))

        def ps(name, shape):
            return ctx.enter_context(nc.psum_tensor(name, shape, F32))

        def sem(name):
            return ctx.enter_context(nc.semaphore(name))

        def dram(name, shape, dt=F32):
            return nc.dram_tensor(name, shape, dt, kind="Internal").ap()

        tables = [x_in, dram("tab1", [NP, D]), dram("tab2", [NP, H]), dram("tab3", [NP, D]), dram("tab4", [NP, D])]
        width = [D, D, H, D, D]
        sums = [dram(f"sums{k}", [EP, width[k]]) for k in range(5)]
        radial_d = dram("radial", [P, T * P], BF16)
        marks = dram("marks", [P, T * D])
        marks_rows = marks.rearrange("p (t f) -> (p t) f", f=D)

        cs = sb("cs", [P, BIG])
        ident, tri, before, iota = (cs[:, k * P:(k + 1) * P] for k in range(4))
        rows_of = [cs[:, 4 * P + k:4 * P + k + 1] for k in range(3)]
        edge0 = cs[:, 4 * P + 3:4 * P + 4]
        iota_b = sb("iota_b", [P, P], BF16)
        zero_b = sb("zero_b", [P, P], BF16)
        ones = sb("ones", [P, P])
        mask = sb("mask", [P, T])
        wgt = sb("wgt", [P, T])
        unit = sb("unit", [P, T * 3])
        big = sb("big", [P, 16640])
        grows = sb("grows", [P, 4 * C3 * D])
        idx = sb("idx", [P, 2 * C], I32)
        xs = sb("xs", [P, NT * D])
        own = sb("own", [P, NT * H])
        agg = sb("agg", [P, NT * H])
        carry = sb("carry", [P, H])
        fix = sb("fix", [P, H])
        filled = sb("filled", [P, D])
        same = sb("same", [P, P])
        firstd = sb("firstd", [P, 1])
        lastd = sb("lastd", [P, 1])
        ends = sb("ends", [P, NT], I32)
        starts = sb("starts", [P, NT], I32)
        first_i = sb("first_i", [P, 1], I32)
        firstx = sb("firstx", [P, D])
        zero = sb("zero", [P, T3 * D])
        end1 = sb("end1", [P, 1], I32)
        stat = sb("stat", [P, 8 * NT])
        posm = sb("posm", [P, NT])
        dinv = sb("dinv", [P, NT])
        blk1 = sb("blk1", [64, 96])
        blk2 = sb("blk2", [96, 96])
        blkl = sb("blkl", [96, 64])
        blk3 = sb("blk3", [64, 64])
        bias = sb("bias", [P, 2 * H + 2 * D])
        bias1, bias2 = bias[:, 0:H], bias[:, H:2 * H]
        biasl, bias3 = bias[:, 2 * H:2 * H + D], bias[:, 2 * H + D:]
        rw1 = sb("rw1", [10, P])
        rw1s = sb("rw1s", [10, RAD])
        wsp = sb("wsp", [P, 896], BF16)

        dstf = big[:, 0:T]
        dsti = big[:, T:2 * T].bitcast(I32)
        tmpi = big[:, 2 * T:3 * T].bitcast(I32)
        b_lo = big[:, 2 * T + T:3 * T + T // 2].bitcast(BF16)
        b_hi = big[:, 3 * T + T // 2:4 * T].bitcast(BF16)
        o = 4 * T
        onelo = [big[:, o + h * C * P // 2:o + (h + 1) * C * P // 2].bitcast(BF16) for h in range(2)]
        o += C * P
        onehi = [big[:, o + h * C * NT // 2:o + (h + 1) * C * NT // 2].bitcast(BF16) for h in range(2)]
        w8 = big[:, 13000:13896]
        wc = big[:, 13896:14792]
        wb1 = big[:, 14792:15240].bitcast(BF16)
        wb2 = big[:, 15240:15688].bitcast(BF16)
        QC = C // 4
        emb = [big[0:10, h * QC * QE:(h + 1) * QC * QE] for h in range(2)]
        hres = [big[:, 2 * QC * QE + k * QE:2 * QC * QE + (k + 1) * QE] for k in range(2)]
        o = 2 * QC * QE + 2 * QE
        hspl = [big[:, o + h * QC * QE // 2:o + (h + 1) * QC * QE // 2].bitcast(BF16) for h in range(2)]
        o += QC * QE
        hmid = big[:, o:o + QE // 2].bitcast(BF16)
        stage_in = [big[:, k:k + NB * H] for k in (0, 10240)]
        stage_T = big[:, 1024:1024 + 7 * P]
        work = big[:, 2048:2048 + NT * D]
        own48 = big[:, 5248:5248 + NT * H]
        rad = [big[:, h * C3 * P // 2:(h + 1) * C3 * P // 2].bitcast(BF16) for h in range(2)]
        o = C3 * P
        prod = [big[:, o + k * G3 * MUL * 72:o + (k + 1) * G3 * MUL * 72] for k in range(2)]
        o += 2 * G3 * MUL * 72
        prod += [a[:, 1248:1248 + G3 * MUL * 72] for a in (agg, own)]
        xsc = [big[:, o + h * C3 * 80:o + h * C3 * 80 + C3 * 16] for h in range(2)]
        pr = [big[:, o + h * C3 * 80 + C3 * 16:o + h * C3 * 80 + C3 * 32] for h in range(2)]
        xsp = [big[:, o + h * C3 * 80:o + h * C3 * 80 + C3 * 32] for h in range(2)]
        xve = [big[:, o + h * C3 * 80 + C3 * 32:o + (h + 1) * C3 * 80] for h in range(2)]
        o += 2 * C3 * 80
        pm = big[:, o:o + C3 * 48]
        o += C3 * 48
        red = [agg[:, k * B3 * VC:(k + 1) * B3 * VC] for k in range(4)]
        rest = [agg[:, 4 * B3 * VC + k * B3 * RC:4 * B3 * VC + (k + 1) * B3 * RC] for k in range(4)]
        sc = [own[:, k * B3 * 24:(k + 1) * B3 * 24] for k in range(4)]
        th = [own[:, (96 + k * 16) * B3:(112 + k * 16) * B3] for k in range(4)]
        vec = [own[:, (160 + k * 24) * B3:(184 + k * 24) * B3] for k in range(2)]
        msg = big[:, o:o + T3 * D]
        o += T3 * D
        assert o <= 16640, o
        rsrc = [grows[:, h * C3 * D:(h + 1) * C3 * D] for h in range(2)]
        rdst = grows[:, T3 * D:2 * T3 * D]

        pair = [ps(f"pair{k}", [P, 1024]) for k in range(2)]
        bank = [pair[0][:, 0:512], pair[0][:, 512:1024], pair[1][:, 0:512], pair[1][:, 512:1024]]
        bank += [ps(f"bank{k}", [P, 512])[:, :] for k in range(4, 8)]
        hist = bank[0][:, 0:NT]

        s_cst, s_small, s_dst, s_ea, s_w8, s_x, s_bias = (sem(n) for n in (
            "s_cst", "s_small", "s_dst", "s_ea", "s_w8", "s_x", "s_bias"))
        s_vector_chain = sem("vector_chain")
        s_blocks_zeroed, s_blocks_in = sem("blocks_zeroed"), sem("blocks_loaded")
        s_square, s_root = sem("square_ready"), sem("root_ready")
        s_len, s_len_root = sem("lengths_squared"), sem("lengths_ready")
        s_idx_in = [[sem(f"idx_in{k}{h}") for h in range(2)] for k in range(5)]
        s_rows_in = [[sem(f"rows_in{k}{h}") for h in range(2)] for k in range(5)]
        s_scan = [sem(f"scanned{k}") for k in range(5)]
        s_sums_out = [[sem(f"sums_out{k}{h}") for h in range(2)] for k in range(5)]
        s_table_out = sem("table_out")
        s_fixmm, s_fixin, s_fixsum, s_fixout = (sem(n) for n in (
            "carry_summed", "fix_rows_in", "fix_added", "fix_rows_out"))
        s_node_rows_in = [sem(f"node_rows_in{b}") for b in range(NBLK)]
        s_ends = sem("ends_ready")
        s_onehot, s_hist, s_hist_zero = sem("onehot_ready"), sem("hist_done"), sem("hist_first")
        s_counts, s_prefix = sem("counts_ready"), sem("prefix_done")
        s_diag, s_diag_mm = sem("diag_ready"), sem("diag_done")
        s_stage, s_transposed, s_transposed_copied, s_stage_mm = sem("stage_in"), sem("transposed"), sem("transposed_copied"), sem("stage_mm")
        s_emb_in = [sem("emb_in0"), sem("emb_in1")]
        s_h_mm, s_h_act, s_h_split, s_h_out = sem("h_mm"), sem("h_act"), sem("h_split"), [sem("h_out0"), sem("h_out1")]
        s_table_ready = sem("table_ready")
        s_radial_in = [sem("rad_in0"), sem("rad_in1")]
        s_weights_mm, s_vec_products, s_act_products, s_reduced = (sem(n) for n in ("weights_mm", "vector_products", "scalar_products", "reduced"))
        s_reduced_copied, s_scalars, s_tanh, s_messages = (sem(n) for n in ("reduced_copied", "scalars_summed", "tanh_ready", "messages_made"))
        s_split, s_channel_sums, s_filled = sem("rows_split"), sem("channels_summed"), sem("destinations_filled")
        s_zeroed, s_mark, s_first, s_zero_ready = sem("marks_zeroed"), sem("marks_out"), sem("first_in"), sem("zero_ready")
        s_marks_in = sem("marks_in")
        s_gpsimd_chain, s_projected, s_gain = sem("gpsimd_chain"), sem("projected"), sem("gain_ready")
        s_gate = {e: sem(f"gate_{e}") for e in ("pool", "sp", "act", "pe", "dve")}

        def gate(eng, who, s, v):
            eng.wait_ge(s, v)
            eng.sem_inc(s_gate[who], 1)

        block = ctx.enter_context(nc.Block())

        def rows(ap, k):
            return ap.rearrange("p (t f) -> p t f", f=k)

        sums_v = [s.rearrange("(p t) f -> p (t f)", p=P) for s in sums]

        @block.sync
        def _(sp):
            def first_idx(k):
                for h in range(2):
                    sp.dma_start(idx[:, h * C:(h + 1) * C], src[:, h * C:(h + 1) * C]).then_inc(s_idx_in[k][h], 16)

            first_idx(0)
            sp.dma_start(cs[:, :], cst).then_inc(s_cst, 16)
            sp.dma_start(dsti, dst).then_inc(s_dst, 16)
            sp.dma_start(wgt[:, :], ew).then_inc(s_ea, 16)
            sp.dma_start(unit[:, :], ea3).then_inc(s_ea, 16)
            for g in range(8):
                sp.dma_start(w8[g * RAD:(g + 1) * RAD, :], R2).then_inc(s_w8, 16)
            sp.dma_start(rw1s[:, :], R1).then_inc(s_small, 16)
            sp.dma_start(rows(xs[:, :], D), x_in.rearrange("(j p) f -> p j f", p=P)).then_inc(s_x, 16)
            for b, s in ((b1, bias1), (b2, bias2), (bl, biasl), (b3, bias3)):
                sp.dma_start(s, b.to_broadcast([P, b.shape[1]])).then_inc(s_bias, 16)
            sp.wait_ge(s_blocks_zeroed, 1)
            for m, W, fi, fo in ((blk1, W1, D, H), (blk2, W2, H, H), (blkl, Wl, H, D), (blk3, W3T, D, D)):
                for q in range(2):
                    sp.dma_start(m[q * fi:(q + 1) * fi, q * fo:(q + 1) * fo], W).then_inc(s_blocks_in, 16)

            def pass_traffic(k, f):
                half = C * f
                if k == 2:
                    sp.wait_ge(s_zero_ready, 1)
                if k:
                    first_idx(k)

                def turn(i, last):
                    for h in range(2):
                        gate(sp, "sp", s_scan[k], 2 * i + h + 1)
                        sp.dma_start(sums_v[k][:, bass.ds((2 * i + h) * half, half)],
                                     grows[:, h * half:(h + 1) * half]).then_inc(s_sums_out[k][h], 16)
                        if not last:
                            sp.dma_start(idx[:, h * C:(h + 1) * C],
                                         src[:, bass.ds((2 * i + 2 + h) * C, C)]).then_inc(s_idx_in[k][h], 16)
                        if k == 2 and h == 0:
                            sp.dma_start(marks[:, bass.ds(i * (T3 * D), T3 * D)], zero[:, :]).then_inc(s_zeroed, 16)
                        if k == 1:
                            gate(sp, "sp", s_h_split, QC * (2 * i + h + 1))
                            sp.dma_start(radial_d[:, bass.ds((2 * i + h) * (C * P), C * P)], hspl[h]).then_inc(s_h_out[h], 16)
                            if not last:
                                sp.dma_start(emb[h], ea10[:, bass.ds((2 * i + 2 + h) * (C * P), C * P)]).then_inc(s_emb_in[h], 16)

                if k == 1:
                    for h in range(2):
                        sp.dma_start(emb[h], ea10[:, h * C * P:(h + 1) * C * P]).then_inc(s_emb_in[h], 16)
                with sp.Fori(0, NIT - 1) as i:
                    turn(i, False)
                turn(NIT - 1, True)

            def blocks_out(k, dest, source, f):
                dest_v, source_v = dest.rearrange("(j p) f -> p j f", p=P), rows(source, f)
                with sp.Fori(0, NBLK) as b:
                    gate(sp, "sp", s_table_ready, k * NBLK + b + 1)
                    sp.dma_start(dest_v[:, bass.ds(b * NB, NB), :], source_v[:, bass.ds(b * NB, NB), :]).then_inc(s_table_out, 16)

            for k in range(PASSES):
                if k == 4:
                    def load_idx(i, h):
                        sp.dma_start(idx[:, h * C3:(h + 1) * C3], src[:, bass.ds(i * T3 + h * C3, C3)]).then_inc(s_idx_in[4][h], 16)

                    def load_marks(i):
                        sp.dma_start(rdst, marks[:, bass.ds(i * (T3 * D), T3 * D)]).then_inc(s_marks_in, 16)

                    def load_rad(i, h):
                        sp.dma_start(rad[h], radial_d[:, bass.ds(i * (T3 * P) + h * C3 * P, C3 * P)]).then_inc(s_radial_in[h], 16)

                    def store(i):
                        gate(sp, "sp", s_scan[4], i + 1)
                        sp.dma_start(sums_v[4][:, bass.ds(i * (T3 * D), T3 * D)], msg).then_inc(s_sums_out[4][0], 16)

                    def turn(i, prev, more, more2):
                        if more:
                            gate(sp, "sp", s_split, 2 * i + 2 + TOKENS)
                            load_idx(i + 1, 1)
                            load_marks(i + 1)
                        if prev:
                            store(i - 1)
                        if more:
                            gate(sp, "sp", s_vec_products, i * T3 + C3)
                            load_rad(i + 1, 0)
                        if more2:
                            gate(sp, "sp", s_split, 2 * i + 3 + TOKENS)
                            load_idx(i + 2, 0)
                        if more:
                            gate(sp, "sp", s_vec_products, i * T3 + T3)
                            load_rad(i + 1, 1)

                    for h in range(2):
                        load_idx(0, h)
                        load_rad(0, h)
                    sp.wait_ge(s_mark, 16 * NT)
                    load_marks(0)
                    gate(sp, "sp", s_split, 1 + TOKENS)
                    load_idx(1, 0)
                    turn(0, False, True, True)
                    with sp.Fori(1, NIT3 - 2) as i:
                        turn(i, True, True, True)
                    turn(NIT3 - 2, True, True, False)
                    turn(NIT3 - 1, True, False, False)
                    store(NIT3 - 1)
                else:
                    pass_traffic(k, width[k])
                if k == PASSES - 1:
                    blocks_out(k, out, xs[:, :], D)
                else:
                    next_table = (own[:, 0:NT * D], own48, own[:, 0:NT * D], xs[:, :])[k]
                    blocks_out(k, tables[k + 1], next_table, width[k + 1])
            sp.wait_ge(s_table_out, 16 * NBLK * PASSES)

        @block.gpsimd
        def _(pool):
            for k in range(PASSES):
                f = width[k]
                if k:
                    pool.wait_ge(s_table_out, 16 * NBLK * k)
                if k < 4:
                    def turn(i, first):
                        for h in range(2):
                            gate(pool, "pool", s_idx_in[k][h], 16 * i + 16)
                            if not first:
                                gate(pool, "pool", s_sums_out[k][h], 16 * i)
                            for j in range(C):
                                pool.indirect_dma_start(
                                    grows[:, (h * C + j) * f:(h * C + j + 1) * f], None, tables[k],
                                    bass.IndirectOffsetOnAxis(idx[:, h * C + j:h * C + j + 1], 0)).then_inc(s_rows_in[k][h], 16)
                    turn(0, True)
                    with pool.Fori(1, NIT) as i:
                        turn(i, False)
                    turns = NIT
                else:
                    pool.indirect_dma_start(firstx[:, :], None, tables[4],
                                            bass.IndirectOffsetOnAxis(first_i[:, 0:1], 0)).then_inc(s_first, 16)
                    def gathers(i, h, js):
                        if js and js[0] == 0:
                            gate(pool, "pool", s_idx_in[4][h], 16 * i + 16)
                            gate(pool, "pool", s_split, 2 * i + h - 1 + TOKENS)
                        for j in js:
                            pool.indirect_dma_start(
                                rsrc[h][:, j * D:(j + 1) * D], None, tables[4],
                                bass.IndirectOffsetOnAxis(idx[:, h * C3 + j:h * C3 + j + 1], 0)).then_inc(s_rows_in[4][h], 16)

                    def project(i, h):
                        gate(pool, "pool", s_split, 2 * i + h + 1 + TOKENS)
                        xv = xve[h].rearrange("p (t u i) -> p t u i", u=MUL, i=3)
                        nv = rows(unit[:, bass.ds(i * (T3 * 3) + h * C3 * 3, C3 * 3)], 3)
                        to = rows(pr[h], MUL)
                        for c in range(3):
                            ch.inc(pool.tensor_tensor(rows(pm[:, c * C3 * MUL:(c + 1) * C3 * MUL], MUL), xv[:, :, :, c],
                                                      bc(nv[:, :, c], 2, MUL), ALU.mult))
                        ch.sync()
                        ch.inc(pool.tensor_tensor(pr[h], pm[:, 0:C3 * MUL], pm[:, C3 * MUL:2 * C3 * MUL], ALU.add))
                        ch.sync()
                        pool.tensor_tensor(pr[h], pr[h], pm[:, 2 * C3 * MUL:3 * C3 * MUL], ALU.add).then_inc(s_projected, 1)

                    def messages(i, b, wait):
                        n = NB3 * i + b
                        r, s_, t_, e_ = (rows(a[b % len(a)], w) for a, w in ((red, VC), (sc, 24), (th, 16), (vec, 24)))
                        mg = rows(msg, D)[:, b * B3:(b + 1) * B3, :]
                        mv = mg[:, :, 8:32].rearrange("p t (w i) -> p t i w", i=3)
                        e4 = e_.rearrange("p t (i w) -> p t i w", i=3)
                        nb = rows(unit[:, bass.ds(i * (T3 * 3) + b * B3 * 3, B3 * 3)], 3)
                        wv = wgt[:, bass.ds(i * T3 + b * B3, B3)]
                        gate(pool, "pool", s_channel_sums, GB * (n + 1) + TOKENS)
                        if wait:
                            gate(pool, "pool", s_sums_out[4][0], 16 * i)
                        gate(pool, "pool", s_tanh, n + 1)
                        ch.inc(pool.tensor_tensor(mg[:, :, 0:8], t_[:, :, 0:8], bc(wv, 2, 8), ALU.mult))
                        ch.inc(pool.tensor_tensor(t_[:, :, 8:16], t_[:, :, 8:16], bc(wv, 2, 8), ALU.mult))
                        ch.inc(pool.tensor_tensor(e4, bc(s_[:, :, 16:24], 2, 3), bc(nb, 3, 8), ALU.mult))
                        ch.sync()
                        ch.inc(pool.tensor_tensor(e_[:, :, 0:VC], e_[:, :, 0:VC], r, ALU.add))
                        ch.inc(pool.tensor_tensor(e_[:, :, VC:24], e_[:, :, VC:24], rows(rest[b % 4], RC), ALU.add))
                        ch.sync()
                        pool.tensor_tensor(mv, e4, bc(t_[:, :, 8:16], 2, 3), ALU.mult).then_inc(s_messages, 1)

                    def turn(i, first, last):
                        done = 0
                        for b in range(NB3):
                            h = b // (NB3 // 2)
                            js = list(range(done % C3, done % C3 + sum(GATHERS[b])))
                            done += sum(GATHERS[b])
                            prev = not (first and b == 0)
                            ib, bb = (i, b - 1) if b else (i - 1, NB3 - 1)
                            if not last:
                                gathers(i + 1, h, js[:GATHERS[b][0]])
                            if b == 1:
                                project(i, 1)
                            if prev:
                                messages(ib, bb, b == 1 and not first)
                            if b == NB3 - 2 and not last:
                                project(i + 1, 0)
                            if not last:
                                gathers(i + 1, h, js[GATHERS[b][0]:])

                    ch = Chain(pool, s_gpsimd_chain)
                    gathers(0, 0, list(range(C3)))
                    pool.wait_ge(s_gain, 1)
                    project(0, 0)
                    gathers(0, 1, list(range(C3)))
                    turn(0, True, False)
                    with pool.Fori(1, NIT3 - 1) as i:
                        ch.enter(i - 1, 5 * NB3 + 2 * 4)
                        turn(i, False, False)
                    ch.leave(NIT3 - 2)
                    turn(NIT3 - 1, False, True)
                    messages(NIT3 - 1, NB3 - 1, False)
                    turns = NIT3
                for h in range(1 if k == 4 else 2):
                    pool.wait_ge(s_sums_out[k][h], 16 * turns)
                if k == 0:
                    pool.wait_ge(s_ends, 1)
                pool.indirect_dma_start(fix[:, 0:f], None, sums[k], bass.IndirectOffsetOnAxis(end1[:, 0:1], 0)).then_inc(s_fixin, 16)
                pool.wait_ge(s_fixsum, k + 1)
                pool.indirect_dma_start(sums[k], bass.IndirectOffsetOnAxis(end1[:, 0:1], 0), fix[:, 0:f], None).then_inc(s_fixout, 16)
                pool.wait_ge(s_fixout, 16 * (k + 1))
                if k == 0:
                    pool.wait_ge(s_ends, 2)
                for j in range(NT):
                    pool.indirect_dma_start(agg[:, j * f:(j + 1) * f], None, sums[k],
                                            bass.IndirectOffsetOnAxis(ends[:, j:j + 1], 0)).then_inc(s_node_rows_in[j // NB], 16)
                if k == 3:
                    pool.wait_ge(s_zeroed, 16 * NIT)
                    for j in range(NT):
                        if j % NB == 0:
                            pool.wait_ge(s_table_ready, k * NBLK + j // NB + 1)
                        pool.indirect_dma_start(marks_rows, bass.IndirectOffsetOnAxis(starts[:, j:j + 1], 0),
                                                xs[:, j * D:(j + 1) * D], None,
                                                bounds_check=EP - 1, oob_is_err=False).then_inc(s_mark, 16)

        @block.scalar
        def _(act):
            roots = 0

            for k in range(PASSES):
                if k == 0:
                    act.wait_ge(s_square, roots + 1)
                    act.activation(stat[:, NT:2 * NT], stat[:, 0:NT], ACT.Sqrt).then_inc(s_root, 1)
                    roots += 1
                if k == 1:
                    def turn(i, first):
                        for h in range(2):
                            if not first:
                                gate(act, "act", s_h_out[h], 16 * i)
                            for q in range(QC):
                                n = (2 * i + h) * QC + q
                                gate(act, "act", s_h_mm, n + 1)
                                pb = bank[2 + (h * QC + q) % 2][:, :]
                                act.activation(hspl[h][:, q * QE:(q + 1) * QE], pb, ACT.Relu, scale=RADIAL_SCALE).then_inc(s_h_act, 1)
                                if not (first and h == 0 and q < 2):
                                    gate(act, "act", s_h_split, n - 1)
                                act.activation(hres[(h * QC + q) % 2], pb, ACT.Relu, scale=RADIAL_SCALE).then_inc(s_h_act, 1)
                    turn(0, True)
                    with act.Fori(1, NIT) as i:
                        turn(i, False)
                if k == 3:
                    with act.Fori(0, 2 * NIT) as i:
                        gate(act, "act", s_len, i + 1)
                        act.activation(big[:, 12000 + C:12000 + 2 * C], big[:, 12000:12000 + C], ACT.Sqrt).then_inc(s_len_root, 1)
                if k == 4:
                    act.sem_inc(s_split, TOKENS)
                    act.sem_inc(s_reduced_copied, TOKENS)

                    def compact(i, h, wait, part):
                        if part == 0:
                            gate(act, "act", s_rows_in[4][h], 16 * C3 * (i + 1))
                            if h == 0:
                                gate(act, "act", s_filled, i + 1)
                            if wait:
                                gate(act, "act", s_vec_products, i * T3 + h * C3 - C3)
                                gate(act, "act", s_act_products, i * T3 + h * C3 - C3)
                        q = part // 2
                        g = rows((rsrc[h], rdst[:, h * C3 * D:(h + 1) * C3 * D])[q], D)
                        if part % 2 == 0:
                            act.copy(rows(xsc[h], 16)[:, :, q * 8:q * 8 + 8], g[:, :, 0:8])
                        else:
                            last = act.copy(rows(xve[h], 48)[:, :, q * 24:q * 24 + 24], g[:, :, 8:32])
                        if part == 3:
                            last.then_inc(s_split, 1)

                    def batch(i, b):
                        n = NB3 * i + b
                        gate(act, "act", s_scalars, n + 1)
                        if not (isinstance(i, int) and n < 4):
                            gate(act, "act", s_messages, n - 3)
                        act.copy(rows(red[b % 4], VC), rows(bank[4 + b % 2][:, 0:B3 * PC], PC)[:, :, 48:PC]).then_inc(s_reduced_copied, 1)
                        act.activation(rows(th[b % 4], 16), rows(sc[b % 4], 24)[:, :, 0:16], ACT.Tanh).then_inc(s_tanh, 1)

                    def products(i, t):
                        h, th_ = t // C3, t % C3
                        pk = prod[t // G3 % 4][:, t % G3 * MUL * 72:(t % G3 + 1) * MUL * 72].rearrange("p (u c) -> p u c", c=72)
                        if th_ == 0:
                            gate(act, "act", s_projected, 2 * i + h + 1)
                            gate(act, "act", s_split, 2 * i + h + 1 + TOKENS)
                        gate(act, "act", s_weights_mm, i * T3 + t + 1)
                        share = bank[6 + t % 2][:, 0:2 * AU * 24].rearrange("p (a x) -> p a x", a=2)
                        for u in range(MUL - AU, MUL):
                            for a, xp in enumerate((xsc[h], pr[h])):
                                last = act.activation(pk[:, u, a * 24:a * 24 + 24], share[:, a, (u - MUL + AU) * 24:(u - MUL + AU) * 24 + 24],
                                                      ACT.Copy, scale=xp[:, th_ * MUL + u:th_ * MUL + u + 1])
                        last.then_inc(s_act_products, 1)

                    def turn(i, first, last):
                        for t in range(T3):
                            products(i, t)
                            b, at = divmod(t - SUM_AT - 1, B3)
                            if at == 0 and b > 0:
                                batch(i, b - 1)
                            elif at == 0 and not first:
                                batch(i - 1, NB3 - 1)
                            if XC1_AT <= t < XC1_AT + 4:
                                compact(i, 1, not first, t - XC1_AT)
                            if XC0_AT <= t < XC0_AT + 4 and not last:
                                compact(i + 1, 0, True, t - XC0_AT)

                    for part in range(4):
                        compact(0, 0, False, part)
                    turn(0, True, False)
                    with act.Fori(1, NIT3 - 1) as i:
                        turn(i, False, False)
                    turn(NIT3 - 1, False, True)
                    batch(NIT3 - 1, NB3 - 1)
                with act.Fori(0, NBLK) as b:
                    for s, st in enumerate(STAGES[k]):
                        fi = 2 * FI[st]
                        gate(act, "act", s_transposed, STAGE_NO[k] + b * len(STAGES[k]) + s + 1)
                        act.copy(stage_T[0:fi, 0:4 * P], bank[0][0:fi, :])
                        act.copy(stage_T[0:fi, 4 * P:7 * P], bank[1][0:fi, 0:3 * P]).then_inc(s_transposed_copied, 1)
                    if k in NORMED:
                        gate(act, "act", s_square, b + (roots + 1))
                        act.activation(stat[:, bass.ds(b * NB + NT, NB)], stat[:, bass.ds(b * NB, NB)], ACT.Sqrt).then_inc(s_root, 1)
                if k in NORMED:
                    roots += NBLK

        @block.vector
        def _(v):
            ch = Chain(v, s_vector_chain)
            TT, TS = v.tensor_tensor, v.tensor_scalar

            def step(ins):
                ch.inc(ins)
                ch.sync()

            for m in (blk1, blk2, blkl, blk3):
                last = v.memset(m[:, :], 0.0)
            ch.inc(last)
            ch.sync()
            v.sem_inc(s_blocks_zeroed, 1)
            v.wait_ge(s_cst, 16)
            v.wait_ge(s_dst, 16)
            step(v.tensor_copy(dstf, dsti))
            v.tensor_copy(iota_b[:, :], iota)
            v.memset(mask[:, 0:1], 0.0)
            v.tensor_copy(firstd[:, :], dstf[:, 0:1])
            v.tensor_copy(first_i[:, :], dsti[:, 0:1])
            v.memset(zero[:, :], 0.0).then_inc(s_zero_ready, 1)
            v.tensor_copy(lastd[:, :], dstf[:, T - 1:T])
            TT(mask[:, 1:T], dstf[:, 1:T], dstf[:, 0:T - 1], ALU.is_equal)
            step(v.tensor_single_scalar(tmpi, dsti, 7, ALU.logical_shift_right))
            step(v.tensor_copy(b_hi, tmpi))
            step(v.tensor_single_scalar(tmpi, dsti, 127, ALU.bitwise_and))
            step(v.tensor_copy(b_lo, tmpi))
            step(TS(agg[:, 0:T], dstf, firstd[:, 0:1], None, ALU.is_equal))
            step(v.tensor_reduce(stat[:, 0:1], agg[:, 0:T], axis=AX.X, op=ALU.add))
            step(TS(stat[:, 1:2], stat[:, 0:1], edge0, -1.0, ALU.add, ALU.add))
            v.tensor_copy(end1[:, :], stat[:, 1:2])
            step(TS(same[:, :], ident, firstd[:, 0:1], None, ALU.mult))
            v.memset(ones[:, :], 1.0).then_inc(s_diag, 1)
            v.wait_ge(s_diag_mm, 1)
            step(TS(same[:, :], bank[1][:, 0:P], lastd[:, 0:1], None, ALU.is_equal))
            TT(same[:, :], same[:, :], before, ALU.mult).then_inc(s_ends, 1)
            def refine(y, d, t):
                step(v.reciprocal(y, y))
                step(TT(t, y, y, ALU.mult))
                step(TT(t, t, d, ALU.mult))
                step(TS(t, t, -0.5, 1.5, ALU.mult, ALU.add))
                step(TT(y, y, t, ALU.mult))

            def split_weights():
                v.wait_ge(s_w8, 128)
                wv = w8.rearrange("p (k u w) -> p k u w", k=7, u=MUL)
                ab = wc[:, 0:WA].rearrange("p (u c) -> p u c", c=24)
                pb_ = wc[:, WA:WA + WB].rearrange("p (u c) -> p u c", c=24)
                fv = wc[:, WA + WB:896].rearrange("p (u c) -> p u c", c=8)
                for blk, dest, at, scale in ((0, ab, 0, PW_S), (2, ab, 8, PW_S), (4, ab, 16, PW_V),
                                             (1, pb_, 0, PW_S), (3, pb_, 8, PW_S), (6, pb_, 16, PW_V * 1.5 ** 0.5)):
                    for to, u0, un in ((0, MUL - AU, AU), (AU, 0, MUL - AU)) if dest is pb_ else ((0, 0, MUL),):
                        TS(dest[:, to:to + un, at:at + 8], wv[:, blk, u0:u0 + un, :], scale, None, ALU.mult)
                step(TS(fv, wv[:, 6, :, :], -PW_V * 1.5 ** 0.5 / 3.0, None, ALU.mult))
                step(v.scalar_tensor_tensor(out=fv, in0=wv[:, 5, :, :], scalar=PW_V * INV_SQRT3, in1=fv, op0=ALU.mult, op1=ALU.add))
                step(v.tensor_copy(wb1, wc))
                step(TT(wc, wc, wb1, ALU.subtract))
                step(v.tensor_copy(wb2, wc))
                step(TT(wc, wc, wb2, ALU.subtract))
                step(TS(wsp[:, :], wc, rows_of[2], None, ALU.mult))
                step(v.scalar_tensor_tensor(out=wsp[:, :], in0=wb2, scalar=rows_of[1], in1=wsp[:, :], op0=ALU.mult, op1=ALU.add))
                step(v.scalar_tensor_tensor(out=wsp[:, :], in0=wb1, scalar=rows_of[0], in1=wsp[:, :], op0=ALU.mult, op1=ALU.add))

            len2, length, len_t = (big[:, 12000 + q * C:12000 + (q + 1) * C] for q in range(3))

            def directions(i, h):
                u = unit[:, bass.ds((2 * i + h) * (C * 3), C * 3)]
                sq = big[:, 12000 + 3 * C:12000 + 6 * C]
                step(TT(sq, u, u, ALU.mult))
                v.tensor_reduce(len2, rows(sq, 3), axis=AX.X, op=ALU.add).then_inc(s_len, 1)
                gate(v, "dve", s_len_root, 2 * i + h + 1)
                refine(length, len2, len_t)
                step(TT(rows(u, 3), rows(u, 3), bc(length, 2, 3), ALU.mult))

            v.wait_ge(s_small, 16)
            step(v.tensor_copy(rw1[:, :].rearrange("k (g r) -> k g r", g=8), bc(rw1s[:, :], 1, 8)))
            v.memset(zero_b[:, :], 0.0).then_inc(s_hist_zero, 1)
            v.wait_ge(s_ea, 32)
            roots = 0

            def scans(k, f, rowsbuf, i, h, cols):
                m = mask[:, bass.ds((2 * i + h) * cols, cols)]
                for c in range(f):
                    last = v.tensor_tensor_scan(out=rowsbuf[:, :, c], data0=m, data1=rowsbuf[:, :, c],
                                                initial=carry[:, c:c + 1], op0=ALU.mult, op1=ALU.add)
                step(last)
                step(v.tensor_copy(carry[:, 0:f], rowsbuf[:, cols - 1, :]))
                v.sem_inc(s_scan[k], 1)

            def layer_norm(b):
                nonlocal roots
                x = xs[:, b * NB * D:(b + 1) * NB * D]
                x3, w = rows(x, D), work[:, 0:NB * D]
                var, root, mean, tmp = (stat[:, q * NT + b * NB:q * NT + (b + 1) * NB] for q in range(4))
                step(v.tensor_reduce(mean, x3, axis=AX.X, op=ALU.add))
                step(TS(mean, mean, 1.0 / D, None, ALU.mult))
                step(TT(x3, x3, bc(mean, 2, D), ALU.subtract))
                step(TT(w, x, x, ALU.mult))
                step(v.tensor_reduce(mean, rows(w, D), axis=AX.X, op=ALU.add))
                TS(var, mean, 1.0 / D, EPS, ALU.mult, ALU.add).then_inc(s_square, 1)
                roots += 1
                v.wait_ge(s_root, roots)
                refine(root, var, tmp)
                step(TT(x3, x3, bc(root, 2, D), ALU.mult))

            def dense_start(k, b, s, st):
                fi = FI[st]
                si = rows(stage_in[s][:, 0:NB * fi], fi)
                a = rows(agg[:, b * NB * fi:(b + 1) * NB * fi], fi)
                mine = own48 if st == 1 else own[:, 0:NT * D]
                dv = dinv[:, b * NB:(b + 1) * NB]
                if st == 2:
                    step(v.tensor_copy(si, a))
                else:
                    step(TT(si, a, rows(mine[:, b * NB * fi:(b + 1) * NB * fi], fi), ALU.add))
                    step(TT(si, si, bc(dv, 2, fi), ALU.mult))
                v.sem_inc(s_stage, 1)

            def dense_end(k, b, s, st):
                fo = FO[st]
                dv = dinv[:, b * NB:(b + 1) * NB]
                v.wait_ge(s_stage_mm, STAGE_NO[k] + b * len(STAGES[k]) + s + 1)
                bb = (bias1, bias2, biasl, bias3)[st]
                for bk, c0, cn in ((2 + 2 * s, 0, 8), (3 + 2 * s, 8, 6)):
                    last = TT(rows(work[:, c0 * fo:(c0 + cn) * fo], fo), rows(bank[bk][:, 0:cn * fo], fo), bc(bb, 1, cn), ALU.add)
                step(last)
                w = work[:, 0:NB * fo]
                x = xs[:, b * NB * D:(b + 1) * NB * D]
                if st == 0:
                    step(v.scalar_tensor_tensor(out=w, in0=w, scalar=SLOPE, in1=w, op0=ALU.mult, op1=ALU.max))
                    step(TT(rows(own48[:, b * NB * fo:(b + 1) * NB * fo], fo), rows(w, fo), bc(dv, 2, fo), ALU.mult))
                elif st == 1:
                    step(v.scalar_tensor_tensor(out=agg[:, b * NB * fo:(b + 1) * NB * fo], in0=w, scalar=SLOPE, in1=w,
                                                op0=ALU.mult, op1=ALU.max))
                elif st == 2:
                    step(TT(x, x, w, ALU.add))
                else:
                    step(v.scalar_tensor_tensor(out=x, in0=w, scalar=0.0, in1=x, op0=ALU.max, op1=ALU.add))

            for k in range(PASSES):
                f = width[k]
                step(v.memset(carry[:, :], 0.0))
                if k == 3:
                    split_weights()
                if k < 4:
                    half = C * f

                    def body(i, h):
                        g = rows(grows[:, h * half:(h + 1) * half], f)
                        if k == 3:
                            directions(i, h)
                        v.wait_ge(s_rows_in[k][h], 16 * C * (i + 1))
                        if k == 0:
                            step(TT(g, g, bc(wgt[:, bass.ds((2 * i + h) * C, C)], 2, f), ALU.mult))
                        else:
                            v.sem_inc(s_gate["dve"], 1)
                        scans(k, f, g, i, h, C)
                        if k == 0:
                            gate(v, "dve", s_hist, 2 * i + 1)
                            lo = b_lo[:, bass.ds((2 * i + h) * C, C)]
                            hi = b_hi[:, bass.ds((2 * i + h) * C, C)]
                            TT(onelo[h].rearrange("p (t c) -> p t c", c=P), bc(lo, 2, P), bc(iota_b[:, :], 1, C), ALU.is_equal)
                            TT(onehi[h].rearrange("p (t c) -> p t c", c=NT), bc(hi, 2, NT), bc(iota_b[:, 0:NT], 1, C), ALU.is_equal).then_inc(s_onehot, 1)
                        if k == 1:
                            for q in range(QC):
                                n = (2 * i + h) * QC + q
                                hs = hspl[h][:, q * QE:(q + 1) * QE]
                                hr = hres[(h * QC + q) % 2]
                                v.wait_ge(s_h_act, 2 * n + 2)
                                step(TT(hr, hr, hs, ALU.subtract))
                                step(v.tensor_copy(hmid, hr))
                                v.tensor_copy(hs[32:64, :], hmid[32:64, :])
                                TT(hs[96:128, :], hr[96:128, :], hmid[96:128, :], ALU.subtract).then_inc(s_h_split, 1)

                    per = {0: 6, 1: 2 * (2 + 2 * QC), 2: 4, 3: 2 * (2 + 7)}[k]
                    with v.Fori(0, NIT) as i:
                        ch.enter(i, per)
                        for h in range(2):
                            body(i, h)
                    ch.leave(NIT)
                else:
                    def products(i, t):
                        h, th_ = t // C3, t % C3
                        q = t % 2
                        pk = prod[t // G3 % 4][:, t % G3 * MUL * 72:(t % G3 + 1) * MUL * 72].rearrange("p (u c) -> p u c", c=72)
                        if th_ == 0:
                            gate(v, "dve", s_projected, 2 * i + h + 1)
                        v.wait_ge(s_weights_mm, i * T3 + t + 1)
                        us = MUL - AU
                        TT(pk[:, 0:us, 0:48].rearrange("p u (a c) -> p a u c", a=2),
                           pair[q][:, :].rearrange("p (a x) -> p a x", a=2)[:, :, 0:us * 24].rearrange("p a (u c) -> p a u c", c=24),
                           bc(xsp[h].rearrange("p (a t u) -> p a t u", a=2, u=MUL)[:, :, th_, 0:us], 3, 24), ALU.mult)
                        TT(pk[:, :, 48:72].rearrange("p u (i w) -> p u i w", i=3),
                           bc(bank[2 * q + 1][:, us * 24:us * 24 + WF].rearrange("p (u w) -> p u w", w=8), 2, 3),
                           bc(xve[h][:, th_ * 48:(th_ + 1) * 48].rearrange("p (u i) -> p u i", i=3), 3, 8),
                           ALU.mult).then_inc(s_vec_products, 1)

                    def channel_sum(i, g):
                        b, j = g // GB % 4, g % GB
                        pv = prod[g % 4].rearrange("p (t u c) -> p t c u", t=G3, c=72)[:, :, PC:72, :]
                        if j == 0 and not (isinstance(i, int) and i == 0 and g < 4 * GB):
                            gate(v, "dve", s_messages, NB3 * i + g // GB - 3)
                        v.wait_ge(s_vec_products, i * T3 + (g + 1) * G3)
                        v.tensor_reduce(rows(rest[b][:, j * G3 * RC:(j + 1) * G3 * RC], RC), pv, axis=AX.X, op=ALU.add).then_inc(s_channel_sums, 1)

                    def sum_scalars(i, b):
                        n = NB3 * i + b
                        gate(v, "dve", s_reduced, GB * n + GB)
                        r = rows(bank[4 + b % 2][:, 0:B3 * PC], PC)
                        v.tensor_reduce(rows(sc[b % 4], 24), r[:, :, 0:48].rearrange("p t (a c) -> p t c a", a=2),
                                        axis=AX.X, op=ALU.add).then_inc(s_scalars, 1)

                    def scan_part(i, part):
                        m = mask[:, bass.ds(i * T3, T3)]
                        mr = rows(msg, D)
                        if part == 0:
                            gate(v, "dve", s_messages, NB3 * (i + 1))
                        for c in range(part * SC, part * SC + SC):
                            last = v.tensor_tensor_scan(out=mr[:, :, c], data0=m, data1=mr[:, :, c],
                                                        initial=carry[:, c:c + 1], op0=ALU.mult, op1=ALU.add)
                        if part == D // SC - 1:
                            step(last)
                            step(v.tensor_copy(carry[:, 0:D], mr[:, T3 - 1, :]))
                            v.sem_inc(s_scan[4], 1)

                    def fill_part(i, part):
                        z = rows(rdst, D)
                        m = mask[:, bass.ds(i * T3, T3)]
                        if part == 0:
                            gate(v, "dve", s_marks_in, 16 * i + 16)
                        for c in range(part * FC, part * FC + FC):
                            last = v.tensor_tensor_scan(out=z[:, :, c], data0=m, data1=z[:, :, c],
                                                        initial=filled[:, c:c + 1], op0=ALU.mult, op1=ALU.add)
                        if part == D // FC - 1:
                            step(last)
                            step(v.tensor_copy(filled[:, :], z[:, T3 - 1, :]))
                            v.sem_inc(s_filled, 1)

                    def turn(i, first, last):
                        for t in range(T3):
                            products(i, t)
                            if t and t % G3 == 0:
                                channel_sum(i, t // G3 - 1)
                            elif t == 0 and not first:
                                channel_sum(i - 1, T3 // G3 - 1)
                            b, at = divmod(t - SUM_AT, B3)
                            if at == 0 and b > 0:
                                sum_scalars(i, b - 1)
                            elif at == 0 and not first:
                                sum_scalars(i - 1, NB3 - 1)
                            if not first and SCAN_AT <= t < SCAN_AT + D // SC:
                                scan_part(i - 1, t - SCAN_AT)
                            if not last and FILL_AT <= t < FILL_AT + D // FC:
                                fill_part(i + 1, t - FILL_AT)

                    v.sem_inc(s_channel_sums, TOKENS)
                    TS(wgt[:, :], wgt[:, :], TANH_GAIN, None, ALU.mult).then_inc(s_gain, 1)
                    v.wait_ge(s_marks_in, 16)
                    v.wait_ge(s_first, 16)
                    step(v.memset(filled[:, :], 0.0))
                    step(v.tensor_copy(rows(rdst, D)[:, 0, :], firstx[:, :]))
                    for part in range(D // FC):
                        fill_part(0, part)
                    ch.sync()
                    turn(0, True, False)
                    per = 2 + 2
                    with v.Fori(1, NIT3 - 1) as i:
                        ch.enter(i - 1, per)
                        turn(i, False, False)
                    ch.leave(NIT3 - 2)
                    turn(NIT3 - 1, False, True)
                    channel_sum(NIT3 - 1, T3 // G3 - 1)
                    sum_scalars(NIT3 - 1, NB3 - 1)
                    for part in range(D // SC):
                        scan_part(NIT3 - 1, part)

                if k == 0:
                    v.wait_ge(s_hist, 2 * NIT + 2)
                    cnt = stat[:, 2 * NT:3 * NT]
                    step(v.tensor_copy(cnt, hist))
                    v.sem_inc(s_counts, 1)
                    step(TS(posm[:, :], cnt, 1.0, None, ALU.min))
                    TS(stat[:, 0:NT], cnt, 1.0, None, ALU.add).then_inc(s_square, 1)
                    v.wait_ge(s_prefix, 1)
                    step(v.tensor_copy(stat[:, 3 * NT:4 * NT], bank[1][:, NT:2 * NT]))
                    step(v.memset(stat[:, 5 * NT:6 * NT], 1.0))
                    step(v.tensor_tensor_scan(out=stat[:, 4 * NT:5 * NT], data0=stat[:, 5 * NT:6 * NT], data1=stat[:, 3 * NT:4 * NT],
                                              initial=0.0, op0=ALU.mult, op1=ALU.add))
                    step(TT(stat[:, 4 * NT:5 * NT], stat[:, 4 * NT:5 * NT], stat[:, 3 * NT:4 * NT], ALU.subtract))
                    step(TT(stat[:, 4 * NT:5 * NT], stat[:, 4 * NT:5 * NT], bank[1][:, 0:NT], ALU.add))
                    step(TT(stat[:, 6 * NT:7 * NT], stat[:, 4 * NT:5 * NT], cnt, ALU.subtract))
                    step(v.scalar_tensor_tensor(out=stat[:, 6 * NT:7 * NT], in0=posm[:, :], scalar=-float(2 ** 22),
                                                in1=stat[:, 6 * NT:7 * NT], op0=ALU.mult, op1=ALU.add))
                    step(TS(stat[:, 6 * NT:7 * NT], stat[:, 6 * NT:7 * NT], float(2 ** 22), None, ALU.add))
                    v.tensor_copy(starts[:, :], stat[:, 6 * NT:7 * NT])
                    step(TS(stat[:, 4 * NT:5 * NT], stat[:, 4 * NT:5 * NT], -1.0, 0.0, ALU.add, ALU.max))
                    v.tensor_copy(ends[:, :], stat[:, 4 * NT:5 * NT]).then_inc(s_ends, 1)
                    roots += 1
                    v.wait_ge(s_root, roots)
                    step(v.tensor_copy(dinv[:, :], stat[:, NT:2 * NT]))
                    refine(dinv[:, :], stat[:, 0:NT], stat[:, 5 * NT:6 * NT])
                v.wait_ge(s_fixin, 16 * (k + 1))
                v.wait_ge(s_fixmm, k + 1)
                TT(fix[:, 0:f], fix[:, 0:f], bank[7][:, 0:f], ALU.add).then_inc(s_fixsum, 1)
                if k == 0:
                    v.wait_ge(s_x, 16)
                    v.wait_ge(s_bias, 64)
                if k == 1:
                    for h in range(2):
                        v.wait_ge(s_h_out[h], 16 * NIT)
                def take(b):
                    x = xs[:, b * NB * D:(b + 1) * NB * D]
                    a = agg[:, b * NB * f:(b + 1) * NB * f]
                    v.wait_ge(s_node_rows_in[b], 16 * NB * (k + 1))
                    step(TT(rows(a, f), rows(a, f), bc(posm[:, b * NB:(b + 1) * NB], 2, f), ALU.mult))
                    if k == 0:
                        step(v.scalar_tensor_tensor(out=x, in0=x, scalar=2.0, in1=a, op0=ALU.mult, op1=ALU.add))
                    if k == 4:
                        step(TT(x, x, a, ALU.add))
                    if STAGES[k]:
                        dense_start(k, b, 0, STAGES[k][0])

                ahead = len(STAGES[k]) == 2
                if ahead:
                    take(0)
                for b in range(NBLK):
                    x = xs[:, b * NB * D:(b + 1) * NB * D]
                    if not ahead:
                        take(b)
                    for s, st in enumerate(STAGES[k]):
                        if s:
                            dense_start(k, b, s, st)
                            if b + 1 < NBLK:
                                take(b + 1)
                        dense_end(k, b, s, st)
                    if k in NORMED:
                        layer_norm(b)
                    if k in (0, 2):
                        step(TT(rows(own[:, b * NB * D:(b + 1) * NB * D], D), rows(x, D), bc(dinv[:, b * NB:(b + 1) * NB], 2, D), ALU.mult))
                    v.sem_inc(s_table_ready, 1)

        @block.tensor
        def _(pe):
            pe.wait_ge(s_diag, 1)
            pe.wait_ge(s_cst, 16)
            pe.matmul(bank[1][:, 0:P], ones[:, :], same[:, :], start=True, stop=True).then_inc(s_diag_mm, 1)
            for k in range(PASSES):
                f = width[k]
                if k == 0:
                    pe.wait_ge(s_hist_zero, 1)
                    pe.matmul(hist, zero_b[:, :], zero_b[:, 0:NT], start=True, stop=False).then_inc(s_hist, 1)
                    with pe.Fori(0, NIT) as i:
                        for h in range(2):
                            gate(pe, "pe", s_onehot, 2 * i + h + 1)
                            for j in range(C):
                                last = pe.matmul(hist, onelo[h][:, j * P:(j + 1) * P], onehi[h][:, j * NT:(j + 1) * NT],
                                                 start=False, stop=False)
                            last.then_inc(s_hist, 1)
                    pe.matmul(hist, zero_b[:, :], zero_b[:, 0:NT], start=False, stop=True).then_inc(s_hist, 1)
                    pe.wait_ge(s_counts, 1)
                    cnt = stat[:, 2 * NT:3 * NT]
                    pe.matmul(bank[1][:, 0:NT], tri, cnt, start=True, stop=True)
                    pe.matmul(bank[1][:, NT:2 * NT], ones[:, :], cnt, start=True, stop=True).then_inc(s_prefix, 1)
                if k == 1:
                    def turn(i, first):
                        for h in range(2):
                            gate(pe, "pe", s_emb_in[h], 16 * i + 16)
                            for q in range(QC):
                                n = (2 * i + h) * QC + q
                                if not (first and h == 0 and q < 2):
                                    gate(pe, "pe", s_h_act, 2 * (n - 1))
                                pe.matmul(bank[2 + (h * QC + q) % 2][:, :], rw1[:, :], emb[h][:, q * QE:(q + 1) * QE],
                                          start=True, stop=True).then_inc(s_h_mm, 1)
                    turn(0, True)
                    with pe.Fori(1, NIT) as i:
                        turn(i, False)
                if k == 4:
                    def weights(i, t):
                        h = t // C3
                        if t % C3 == 0:
                            gate(pe, "pe", s_radial_in[h], 16 * i + 16)
                        lt = rad[h][:, (t % C3) * P:(t % C3 + 1) * P]
                        us, ue = (MUL - AU) * 24, (MUL + AU) * 24
                        pe.matmul(bank[6 + t % 2][:, 0:ue - us], lt, wsp[:, us:ue], start=True, stop=True)
                        pe.matmul(bank[2 * (t % 2)][:, 0:us], lt, wsp[:, 0:us], start=True, stop=True)
                        pe.matmul(bank[2 * (t % 2) + 1][:, 0:us + WF], lt, wsp[:, ue:ue + us + WF],
                                  start=True, stop=True).then_inc(s_weights_mm, 1)

                    def reduce(i, g, us):
                        b, j = g // GB, g % GB
                        if j == 0 and us[0] == 0:
                            gate(pe, "pe", s_reduced_copied, NB3 * i + b - 1 + TOKENS)
                        pv = prod[g % 4].rearrange("p (t u c) -> p t u c", t=G3, c=72)[:, :, :, 0:PC]
                        for u in us:
                            last = pe.matmul(bank[4 + b % 2][:, j * G3 * PC:(j + 1) * G3 * PC], ident, pv[:, :, u, :],
                                             start=(u == 0), stop=(u == MUL - 1))
                        if us[-1] == MUL - 1:
                            last.then_inc(s_reduced, 1)

                    parts = (list(range(0, 5)), list(range(5, 11)), list(range(11, MUL)))

                    def turn(i, first, last):
                        for t in range(T3):
                            gate(pe, "pe", s_vec_products, i * T3 + t + 1)
                            gate(pe, "pe", s_act_products, i * T3 + t + 1)
                            if not (last and t + 2 >= T3):
                                if (t + 2) % G3 == 0:
                                    gate(pe, "pe", s_channel_sums, i * (T3 // G3) + (t + 2) // G3 - 2 + TOKENS)
                                weights(*((i, t + 2) if t + 2 < T3 else (i + 1, t + 2 - T3)))
                            if t >= G3 - 1:
                                reduce(i, (t + 1) // G3 - 1, parts[(t + 1) % G3])
                            elif not first:
                                reduce(i - 1, T3 // G3 - 1, parts[t + 1])

                    weights(0, 0)
                    weights(0, 1)
                    turn(0, True, False)
                    with pe.Fori(1, NIT3 - 1) as i:
                        turn(i, False, False)
                    turn(NIT3 - 1, False, True)
                    for us in parts[1:]:
                        reduce(NIT3 - 1, T3 // G3 - 1, us)
                pe.wait_ge(s_scan[k], NIT3 if k == 4 else 2 * NIT)
                pe.matmul(bank[7][:, 0:f], same[:, :], carry[:, 0:f], start=True, stop=True).then_inc(s_fixmm, 1)
                if k == 1:
                    pe.wait_ge(s_blocks_in, 128)
                if STAGES[k]:
                    with pe.Fori(0, NBLK) as b:
                        for s, st in enumerate(STAGES[k]):
                            fi, fo = FI[st], FO[st]
                            n = STAGE_NO[k] + b * len(STAGES[k]) + s
                            gate(pe, "pe", s_stage, n + 1)
                            for q in range(7):
                                last = pe.transpose(bank[q // 4][0:2 * fi, (q % 4) * P:(q % 4 + 1) * P],
                                                    stage_in[s][:, q * 2 * fi:(q + 1) * 2 * fi], ident)
                            last.then_inc(s_transposed, 1)
                            gate(pe, "pe", s_transposed_copied, n + 1)
                            for q in range(7):
                                last = pe.matmul(bank[2 + 2 * s + q // 4][:, (q % 4) * 2 * fo:(q % 4 + 1) * 2 * fo],
                                                 stage_T[0:2 * fi, q * P:(q + 1) * P], (blk1, blk2, blkl, blk3)[st][:, :],
                                                 start=True, stop=True)
                            last.then_inc(s_stage_mm, 1)


def kernel(x, src, dst, edge_attr_10, edge_attr_3, edge_weight, L1_gnn_W1, L1_gnn_b1, L1_gnn_W2, L1_gnn_b2,
           L1_gnn_Wl, L1_gnn_bl, L2_gnn_W, L2_gnn_bias, L3_gnn_W1, L3_gnn_W2):
    import numpy as _np
    import concourse.bacc as _bacc
    from concourse.bass_utils import run_bass_kernel_spmd as _run

    def edges(a, fill):
        a = _np.asarray(a)
        a = _np.concatenate([a, _np.full((EP - E,) + a.shape[1:], fill, a.dtype)])
        return a.reshape((P, T) + a.shape[1:])

    cst = _np.zeros((P, BIG), _np.float32)
    cst[:, 0:P] = _np.eye(P)
    cst[:, P:2 * P] = _np.triu(_np.ones((P, P)))
    cst[:, 2 * P:3 * P] = _np.triu(_np.ones((P, P)), 1)
    cst[:, 3 * P:4 * P] = _np.arange(P)
    parts = [0] * 16 + [1] * 16 + [0] * 16 + [1] * 16 + [2] * 16 + [-1] * 16 + [0] * 16 + [-1] * 16
    for k in range(3):
        cst[:, 4 * P + k] = _np.array([q == k for q in parts])
    cst[:, 4 * P + 3] = _np.arange(P) * T
    x = _np.asarray(x)
    arrays = {
        "x": _np.concatenate([x, _np.zeros((NP - N, D), x.dtype)]),
        "src": edges(src, 0), "dst": edges(dst, N),
        "ea10": _np.ascontiguousarray(edges(edge_attr_10, 0).transpose(2, 1, 0).reshape(10, T * P)),
        "ea3": edges(edge_attr_3, 1).reshape(P, T * 3), "ew": edges(edge_weight, 0),
        "W1": L1_gnn_W1, "b1": _np.asarray(L1_gnn_b1).reshape(1, H), "W2": L1_gnn_W2, "b2": _np.asarray(L1_gnn_b2).reshape(1, H),
        "Wl": L1_gnn_Wl, "bl": _np.asarray(L1_gnn_bl).reshape(1, D), "W3T": _np.ascontiguousarray(_np.asarray(L2_gnn_W).T),
        "b3": _np.asarray(L2_gnn_bias).reshape(1, D), "R1": L3_gnn_W1, "R2": L3_gnn_W2, "cst": cst,
    }
    arrays = {f"in_{n}": _np.ascontiguousarray(a) for n, a in arrays.items()}
    nc = _bacc.Bacc("TRN2", target_bir_lowering=False, num_devices=1)
    args = [nc.dram_tensor(n, a.shape, mybir.dt.from_np(a.dtype), kind="ExternalInput").ap() for n, a in arrays.items()]
    args.append(nc.dram_tensor("out_x", (NP, D), F32, kind="ExternalOutput").ap())
    gnn(nc, *args)
    r = _run(nc, [arrays], core_ids=[0])
    return r.results[0]["out_x"][0:N]
```
